# Optimizing a Trainium2 kernel written in Bass

```python
import numpy as np
import jax
import jax.numpy as jnp

def _softmax(x, axis=-1):
    return jax.nn.softmax(x, axis=axis)

def _gelu(x):
    return jax.nn.gelu(x, approximate=True)

def _silu(x):
    return jax.nn.silu(x)

def _sigmoid(x):
    return jax.nn.sigmoid(x)

def _layernorm(x, axis=-1, eps=1e-05):
    m = jnp.mean(x, axis=axis, keepdims=True)
    v = jnp.var(x, axis=axis, keepdims=True)
    return (x - m) / jnp.sqrt(v + eps)

def _scatter_add(tgt, idx, src, axis=0):
    return tgt.at[idx].add(src)

def _segment_sum(src, seg, n):
    return jax.ops.segment_sum(src, seg, n)
kernel_name = 'mk_adaln_ffn_d4_seqx_r8_2e5187'

def setup_inputs(seed: int=0):
    np.random.seed(seed)
    _w = jnp.asarray

    def _rec_inputs():
        import jax
        import jax.numpy as jnp
        _rk = jax.random.key(seed)
        x = -0.000125 + 0.9999 * jax.random.normal(jax.random.fold_in(_rk, 1), (64, 32, 512), jnp.float32)
        _lenS = 32 - jax.random.randint(jax.random.fold_in(_rk, 7), (64,), 0, max(1, 32 // 4) + 1, jnp.int32)
        _lenS2 = 32 - jax.random.randint(jax.random.fold_in(_rk, 8), (64,), 0, max(1, 32 // 4) + 1, jnp.int32)
        cond_128 = 0.0061147 + 1.02565 * jax.random.normal(jax.random.fold_in(_rk, 11), (64, 128), jnp.float32)
        fside_S_0 = -0.022604 + 0.987366 * jax.random.normal(jax.random.fold_in(_rk, 12), (32,), jnp.float32)
        return (x, cond_128, fside_S_0)
    x, cond_128, fside_S_0 = _rec_inputs()

    def _L0_cond_setup():
        import jax, jax.numpy as jnp
        import numpy as np
        from jax import lax
        N, C_IN, L = (32, 32, 512)
        C_OUT, K, GROUPS = (32, 9, 4)
        C_DIM, PAD, STRIDE = (128, 4, 1)
        key = jax.random.key(seed)
        k1, k2, k3, k4, k5 = jax.random.split(key, 5)
        x = jax.random.normal(k1, (N, C_IN, L), dtype=jnp.float32)
        c = jax.random.normal(k2, (N, C_DIM), dtype=jnp.float32)
        weight = jax.random.normal(k3, (C_OUT, C_IN // GROUPS, K), dtype=jnp.float32)
        c_weight = jax.random.normal(k4, (C_OUT, C_DIM), dtype=jnp.float32)
        bias = jax.random.normal(k5, (C_OUT,), dtype=jnp.float32)
        return {'x': x, 'c': c, 'weight': weight, 'c_weight': c_weight, 'bias': bias}
    _L0_cond_all = _L0_cond_setup()
    _L0_cond_in = {k: v for k, v in _L0_cond_all.items() if k in ('weight', 'c_weight')}
    del _L0_cond_all

    def _L0_ffn_setup():
        import jax, jax.numpy as jnp
        import numpy as np
        N_EXPERTS = 28
        TOP_K = 2
        RANK = 8
        LORA_ALPHA = 16
        SCALING = LORA_ALPHA / RANK
        TEMP = 1.0
        key = jax.random.key(seed)
        ks = jax.random.split(key, 5)
        B, S, D_IN, D_OUT = (4, 256, 512, 512)
        x = jax.random.normal(ks[0], (B, S, D_IN), dtype=jnp.float32)
        base_W = jax.random.normal(ks[1], (D_OUT, D_IN), dtype=jnp.float32) * (1.0 / np.sqrt(D_IN))
        gate_W = jax.random.normal(ks[2], (N_EXPERTS, D_IN), dtype=jnp.float32) * (1.0 / np.sqrt(D_IN))
        lora_A = jax.random.normal(ks[3], (N_EXPERTS, RANK, D_IN), dtype=jnp.float32) * (1.0 / np.sqrt(D_IN))
        lora_B = jax.random.normal(ks[4], (N_EXPERTS, D_OUT, RANK), dtype=jnp.float32) * 0.01
        return {'x': x, 'base_W': base_W, 'gate_W': gate_W, 'lora_A': lora_A, 'lora_B': lora_B}
    _L0_ffn_all = _L0_ffn_setup()
    _L0_ffn_in = {k: v for k, v in _L0_ffn_all.items() if k in ('base_W', 'gate_W', 'lora_A', 'lora_B')}
    del _L0_ffn_all

    def _L1_cond_setup():
        import jax, jax.numpy as jnp
        import numpy as np
        K = 8
        T = 1.0
        D_EMBD = 128
        IN_C = 32
        OUT_C = 32
        BS = 32
        H = 512
        HID = 128
        key = jax.random.key(seed)
        ks = jax.random.split(key, 10)
        s = lambda fan_in: 1.0 / np.sqrt(fan_in)
        return {'x': jax.random.normal(ks[0], (BS, IN_C, H), dtype=jnp.float32), 'embedding': jax.random.normal(ks[1], (BS, D_EMBD), dtype=jnp.float32), 'W0': jax.random.normal(ks[2], (D_EMBD, HID), dtype=jnp.float32) * s(D_EMBD), 'b0': jnp.zeros((HID,), dtype=jnp.float32), 'W1': jax.random.normal(ks[3], (HID, HID), dtype=jnp.float32) * s(HID), 'b1': jnp.zeros((HID,), dtype=jnp.float32), 'W2': jax.random.normal(ks[4], (HID, K), dtype=jnp.float32) * s(HID), 'b2': jnp.zeros((K,), dtype=jnp.float32), 'weight': jax.random.normal(ks[5], (K, OUT_C, IN_C, 1), dtype=jnp.float32) * s(IN_C), 'bias_k': jax.random.normal(ks[6], (K, OUT_C), dtype=jnp.float32) * 0.1}
    _L1_cond_all = _L1_cond_setup()
    _L1_cond_in = {k: v for k, v in _L1_cond_all.items() if k in ('W0', 'b0', 'W1', 'b1', 'W2', 'b2', 'weight', 'bias_k')}
    del _L1_cond_all

    def _L1_ffn_setup():
        import jax, jax.numpy as jnp
        import numpy as np
        N_BITS = 8
        QMAX = float(2 ** (N_BITS - 1) - 1)
        QMIN = -QMAX - 1.0
        EPS = 1e-08

        def _fq(x, scale):
            return jnp.clip(jnp.round(x / scale), QMIN, QMAX) * scale

        def fake_quant_per_token(x):
            max_abs = jnp.max(jnp.abs(x), axis=-1, keepdims=True)
            scale = jnp.maximum(max_abs / QMAX, EPS)
            return _fq(x, scale)

        def fake_quant_per_channel(w):
            max_abs = jnp.max(jnp.abs(w), axis=1, keepdims=True)
            scale = jnp.maximum(max_abs / QMAX, EPS)
            return _fq(w, scale)
        key = jax.random.key(seed)
        kx, kw, kb = jax.random.split(key, 3)
        B, S, D_IN, D_OUT = (4, 256, 512, 512)
        x = jax.random.normal(kx, (B, S, D_IN), dtype=jnp.float32)
        w = jax.random.normal(kw, (D_OUT, D_IN), dtype=jnp.float32) * 0.02
        b = jax.random.normal(kb, (D_OUT,), dtype=jnp.float32) * 0.02
        return {'x': x, 'w': w, 'b': b}
    _L1_ffn_all = _L1_ffn_setup()
    _L1_ffn_in = {k: v for k, v in _L1_ffn_all.items() if k in ('w', 'b')}
    del _L1_ffn_all

    def _L2_cond_setup():
        import jax, jax.numpy as jnp
        import numpy as np
        K = 8
        T = 1.0
        D_EMBD = 128
        IN_C = 32
        OUT_C = 32
        BS = 32
        H = 512
        HID = 128
        key = jax.random.key(seed)
        ks = jax.random.split(key, 10)
        s = lambda fan_in: 1.0 / np.sqrt(fan_in)
        return {'x': jax.random.normal(ks[0], (BS, IN_C, H), dtype=jnp.float32), 'embedding': jax.random.normal(ks[1], (BS, D_EMBD), dtype=jnp.float32), 'W0': jax.random.normal(ks[2], (D_EMBD, HID), dtype=jnp.float32) * s(D_EMBD), 'b0': jnp.zeros((HID,), dtype=jnp.float32), 'W1': jax.random.normal(ks[3], (HID, HID), dtype=jnp.float32) * s(HID), 'b1': jnp.zeros((HID,), dtype=jnp.float32), 'W2': jax.random.normal(ks[4], (HID, K), dtype=jnp.float32) * s(HID), 'b2': jnp.zeros((K,), dtype=jnp.float32), 'weight': jax.random.normal(ks[5], (K, OUT_C, IN_C, 1), dtype=jnp.float32) * s(IN_C), 'bias_k': jax.random.normal(ks[6], (K, OUT_C), dtype=jnp.float32) * 0.1}
    _L2_cond_all = _L2_cond_setup()
    _L2_cond_in = {k: v for k, v in _L2_cond_all.items() if k in ('W0', 'b0', 'W1', 'b1', 'W2', 'b2', 'weight', 'bias_k')}
    del _L2_cond_all

    def _L2_ffn_setup():
        import jax, jax.numpy as jnp
        import numpy as np
        HD, M = (512, 1792)
        key = jax.random.key(seed)
        k_x, k_g, k_u, k_d = jax.random.split(key, 4)
        scale = 1.0 / np.sqrt(HD)
        x = jax.random.normal(k_x, (4, 256, HD), dtype=jnp.float16)
        W_gate = jax.random.normal(k_g, (M, HD), dtype=jnp.float16) * jnp.float16(scale)
        W_up = jax.random.normal(k_u, (M, HD), dtype=jnp.float16) * jnp.float16(scale)
        W_down = jax.random.normal(k_d, (HD, M), dtype=jnp.float16) * jnp.float16(1.0 / np.sqrt(M))
        return {'x': x, 'W_gate': W_gate, 'W_up': W_up, 'W_down': W_down}
    _L2_ffn_all = _L2_ffn_setup()
    _L2_ffn_in = {k: v for k, v in _L2_ffn_all.items() if k in ('W_gate', 'W_up', 'W_down')}
    del _L2_ffn_all

    def _L3_cond_setup():
        import jax, jax.numpy as jnp
        import numpy as np
        K = 8
        T = 1.0
        D_EMBD = 128
        IN_C = 32
        OUT_C = 32
        BS = 32
        H = 512
        HID = 128
        key = jax.random.key(seed)
        ks = jax.random.split(key, 10)
        s = lambda fan_in: 1.0 / np.sqrt(fan_in)
        return {'x': jax.random.normal(ks[0], (BS, IN_C, H), dtype=jnp.float32), 'embedding': jax.random.normal(ks[1], (BS, D_EMBD), dtype=jnp.float32), 'W0': jax.random.normal(ks[2], (D_EMBD, HID), dtype=jnp.float32) * s(D_EMBD), 'b0': jnp.zeros((HID,), dtype=jnp.float32), 'W1': jax.random.normal(ks[3], (HID, HID), dtype=jnp.float32) * s(HID), 'b1': jnp.zeros((HID,), dtype=jnp.float32), 'W2': jax.random.normal(ks[4], (HID, K), dtype=jnp.float32) * s(HID), 'b2': jnp.zeros((K,), dtype=jnp.float32), 'weight': jax.random.normal(ks[5], (K, OUT_C, IN_C, 1), dtype=jnp.float32) * s(IN_C), 'bias_k': jax.random.normal(ks[6], (K, OUT_C), dtype=jnp.float32) * 0.1}
    _L3_cond_all = _L3_cond_setup()
    _L3_cond_in = {k: v for k, v in _L3_cond_all.items() if k in ('W0', 'b0', 'W1', 'b1', 'W2', 'b2', 'weight', 'bias_k')}
    del _L3_cond_all

    def _L3_ffn_setup():
        import jax, jax.numpy as jnp
        import numpy as np
        B, S, D = (4, 256, 512)
        NUM_EXPERTS, TOP_K = (3, 2)

        def _expert_outputs(h, w1, b1, w2, b2):
            pre = jnp.einsum('bsd,edf->ebsf', h, w1) + b1[:, None, None, :]
            act = jnp.stack([jnp.tanh(pre[0]), jax.nn.gelu(pre[1], approximate=False), jax.nn.silu(pre[2])])
            return jnp.einsum('ebsf,efd->ebsd', act, w2) + b2[:, None, None, :]
        key = jax.random.key(seed)
        ks = jax.random.split(key, 8)
        scale_in = 1.0 / np.sqrt(D)
        scale_gate = 1.0 / np.sqrt(D + 1)
        return {'h': jax.random.normal(ks[0], (B, S, D), dtype=jnp.float32), 'gate_w': jax.random.uniform(ks[1], (D + 1, NUM_EXPERTS), minval=-scale_gate, maxval=scale_gate, dtype=jnp.float32), 'gate_b': jnp.zeros((NUM_EXPERTS,), dtype=jnp.float32), 'w1': jax.random.uniform(ks[2], (NUM_EXPERTS, D, D), minval=-scale_in, maxval=scale_in, dtype=jnp.float32), 'b1': jnp.zeros((NUM_EXPERTS, D), dtype=jnp.float32), 'w2': jax.random.uniform(ks[3], (NUM_EXPERTS, D, D), minval=-scale_in, maxval=scale_in, dtype=jnp.float32), 'b2': jnp.zeros((NUM_EXPERTS, D), dtype=jnp.float32)}
    _L3_ffn_all = _L3_ffn_setup()
    _L3_ffn_in = {k: v for k, v in _L3_ffn_all.items() if k in ('gate_w', 'gate_b', 'w1', 'b1', 'w2', 'b2')}
    del _L3_ffn_all
    return {'x': x, 'cond_128': cond_128, 'fside_S_0': fside_S_0, 'L0_cond_weight': _L0_cond_in['weight'], 'L0_cond_c_weight': _L0_cond_in['c_weight'], 'L0_ffn_base_W': _L0_ffn_in['base_W'], 'L0_ffn_gate_W': _L0_ffn_in['gate_W'], 'L0_ffn_lora_A': _L0_ffn_in['lora_A'], 'L0_ffn_lora_B': _L0_ffn_in['lora_B'], 'L1_cond_W0': _L1_cond_in['W0'], 'L1_cond_b0': _L1_cond_in['b0'], 'L1_cond_W1': _L1_cond_in['W1'], 'L1_cond_b1': _L1_cond_in['b1'], 'L1_cond_W2': _L1_cond_in['W2'], 'L1_cond_b2': _L1_cond_in['b2'], 'L1_cond_weight': _L1_cond_in['weight'], 'L1_cond_bias_k': _L1_cond_in['bias_k'], 'L1_ffn_w': _L1_ffn_in['w'], 'L1_ffn_b': _L1_ffn_in['b'], 'L2_cond_W0': _L2_cond_in['W0'], 'L2_cond_b0': _L2_cond_in['b0'], 'L2_cond_W1': _L2_cond_in['W1'], 'L2_cond_b1': _L2_cond_in['b1'], 'L2_cond_W2': _L2_cond_in['W2'], 'L2_cond_b2': _L2_cond_in['b2'], 'L2_cond_weight': _L2_cond_in['weight'], 'L2_cond_bias_k': _L2_cond_in['bias_k'], 'L2_ffn_W_gate': _L2_ffn_in['W_gate'], 'L2_ffn_W_up': _L2_ffn_in['W_up'], 'L2_ffn_W_down': _L2_ffn_in['W_down'], 'L3_cond_W0': _L3_cond_in['W0'], 'L3_cond_b0': _L3_cond_in['b0'], 'L3_cond_W1': _L3_cond_in['W1'], 'L3_cond_b1': _L3_cond_in['b1'], 'L3_cond_W2': _L3_cond_in['W2'], 'L3_cond_b2': _L3_cond_in['b2'], 'L3_cond_weight': _L3_cond_in['weight'], 'L3_cond_bias_k': _L3_cond_in['bias_k'], 'L3_ffn_gate_w': _L3_ffn_in['gate_w'], 'L3_ffn_gate_b': _L3_ffn_in['gate_b'], 'L3_ffn_w1': _L3_ffn_in['w1'], 'L3_ffn_b1': _L3_ffn_in['b1'], 'L3_ffn_w2': _L3_ffn_in['w2'], 'L3_ffn_b2': _L3_ffn_in['b2']}

def reference(x, cond_128, fside_S_0, L0_cond_weight, L0_cond_c_weight, L0_ffn_base_W, L0_ffn_gate_W, L0_ffn_lora_A, L0_ffn_lora_B, L1_cond_W0, L1_cond_b0, L1_cond_W1, L1_cond_b1, L1_cond_W2, L1_cond_b2, L1_cond_weight, L1_cond_bias_k, L1_ffn_w, L1_ffn_b, L2_cond_W0, L2_cond_b0, L2_cond_W1, L2_cond_b1, L2_cond_W2, L2_cond_b2, L2_cond_weight, L2_cond_bias_k, L2_ffn_W_gate, L2_ffn_W_up, L2_ffn_W_down, L3_cond_W0, L3_cond_b0, L3_cond_W1, L3_cond_b1, L3_cond_W2, L3_cond_b2, L3_cond_weight, L3_cond_bias_k, L3_ffn_gate_w, L3_ffn_gate_b, L3_ffn_w1, L3_ffn_b1, L3_ffn_w2, L3_ffn_b2):
    import jax
    import jax.numpy as jnp

    def _L0_cond_ref(x, c, weight, c_weight, bias):
        import jax, jax.numpy as jnp
        import numpy as np
        from jax import lax
        N, C_IN, L = (32, 32, 512)
        C_OUT, K, GROUPS = (32, 9, 4)
        C_DIM, PAD, STRIDE = (128, 4, 1)
        out = lax.conv_general_dilated(x, weight, window_strides=(STRIDE,), padding=[(PAD, PAD)], dimension_numbers=('NCH', 'OIH', 'NCH'), feature_group_count=GROUPS)
        ctx = jnp.einsum('nd,od->no', c, c_weight)
        out = out + ctx[:, :, None] + bias[None, :, None]
        return out

    def _L0_ffn_ref(x, base_W, gate_W, lora_A, lora_B):
        import jax, jax.numpy as jnp
        import numpy as np
        N_EXPERTS = 28
        TOP_K = 2
        RANK = 8
        LORA_ALPHA = 16
        SCALING = LORA_ALPHA / RANK
        TEMP = 1.0
        B, S, D_in = x.shape
        xf = x.reshape(B * S, D_in)
        base = xf @ base_W.T
        logits = xf @ gate_W.T
        top_vals, top_idx = jax.lax.top_k(logits, TOP_K)
        top_probs = jax.nn.softmax(top_vals / TEMP, axis=-1)
        N = xf.shape[0]
        gate_full = jnp.zeros((N, N_EXPERTS), dtype=xf.dtype).at[jnp.arange(N)[:, None], top_idx].add(top_probs)
        h = jnp.einsum('nd,erd->ner', xf, lora_A)
        h = h * (gate_full * SCALING)[:, :, None]
        lora_out = jnp.einsum('ner,eor->no', h, lora_B)
        out = base + lora_out
        return out.reshape(B, S, -1)

    def _L1_cond_ref(x, embedding, W0, b0, W1, b1, W2, b2, weight, bias_k):
        import jax, jax.numpy as jnp
        import numpy as np
        K = 8
        T = 1.0
        D_EMBD = 128
        IN_C = 32
        OUT_C = 32
        BS = 32
        H = 512
        HID = 128
        h = jax.nn.gelu(embedding @ W0 + b0, approximate=False)
        h = jax.nn.gelu(h @ W1 + b1, approximate=False)
        att = jax.nn.softmax((h @ W2 + b2) / T, axis=-1)
        agg_w = jnp.einsum('bk,koi->boi', att, weight[..., 0])
        agg_b = att @ bias_k
        out = jnp.einsum('boi,bih->boh', agg_w, x) + agg_b[:, :, None]
        return out

    def _L1_ffn_ref(x, w, b):
        import jax, jax.numpy as jnp
        import numpy as np
        N_BITS = 8
        QMAX = float(2 ** (N_BITS - 1) - 1)
        QMIN = -QMAX - 1.0
        EPS = 1e-08

        def _fq(x, scale):
            return jnp.clip(jnp.round(x / scale), QMIN, QMAX) * scale

        def fake_quant_per_token(x):
            max_abs = jnp.max(jnp.abs(x), axis=-1, keepdims=True)
            scale = jnp.maximum(max_abs / QMAX, EPS)
            return _fq(x, scale)

        def fake_quant_per_channel(w):
            max_abs = jnp.max(jnp.abs(w), axis=1, keepdims=True)
            scale = jnp.maximum(max_abs / QMAX, EPS)
            return _fq(w, scale)
        w_q = fake_quant_per_channel(w)
        x_q = fake_quant_per_token(x)
        y = jnp.einsum('bsi,oi->bso', x_q, w_q) + b
        return y

    def _L2_cond_ref(x, embedding, W0, b0, W1, b1, W2, b2, weight, bias_k):
        import jax, jax.numpy as jnp
        import numpy as np
        K = 8
        T = 1.0
        D_EMBD = 128
        IN_C = 32
        OUT_C = 32
        BS = 32
        H = 512
        HID = 128
        h = jax.nn.gelu(embedding @ W0 + b0, approximate=False)
        h = jax.nn.gelu(h @ W1 + b1, approximate=False)
        att = jax.nn.softmax((h @ W2 + b2) / T, axis=-1)
        agg_w = jnp.einsum('bk,koi->boi', att, weight[..., 0])
        agg_b = att @ bias_k
        out = jnp.einsum('boi,bih->boh', agg_w, x) + agg_b[:, :, None]
        return out

    def _L2_ffn_ref(x, W_gate, W_up, W_down):
        import jax, jax.numpy as jnp
        import numpy as np
        HD, M = (512, 1792)
        gate = jnp.einsum('bsh,mh->bsm', x, W_gate)
        up = jnp.einsum('bsh,mh->bsm', x, W_up)
        h = jax.nn.silu(gate) * up
        out = jnp.einsum('bsm,hm->bsh', h, W_down)
        return out

    def _L3_cond_ref(x, embedding, W0, b0, W1, b1, W2, b2, weight, bias_k):
        import jax, jax.numpy as jnp
        import numpy as np
        K = 8
        T = 1.0
        D_EMBD = 128
        IN_C = 32
        OUT_C = 32
        BS = 32
        H = 512
        HID = 128
        h = jax.nn.gelu(embedding @ W0 + b0, approximate=False)
        h = jax.nn.gelu(h @ W1 + b1, approximate=False)
        att = jax.nn.softmax((h @ W2 + b2) / T, axis=-1)
        agg_w = jnp.einsum('bk,koi->boi', att, weight[..., 0])
        agg_b = att @ bias_k
        out = jnp.einsum('boi,bih->boh', agg_w, x) + agg_b[:, :, None]
        return out

    def _L3_ffn_ref(h, gate_w, gate_b, w1, b1, w2, b2):
        import jax, jax.numpy as jnp
        import numpy as np
        B, S, D = (4, 256, 512)
        NUM_EXPERTS, TOP_K = (3, 2)

        def _expert_outputs(h, w1, b1, w2, b2):
            pre = jnp.einsum('bsd,edf->ebsf', h, w1) + b1[:, None, None, :]
            act = jnp.stack([jnp.tanh(pre[0]), jax.nn.gelu(pre[1], approximate=False), jax.nn.silu(pre[2])])
            return jnp.einsum('ebsf,efd->ebsd', act, w2) + b2[:, None, None, :]
        b, s, d = h.shape
        vision_len = int(s * 0.3)
        text_strength = jnp.mean(jnp.abs(h[:, vision_len:, :]), axis=(1, 2), keepdims=True)
        vision_strength = jnp.mean(jnp.abs(h[:, :vision_len, :]), axis=(1, 2), keepdims=True)
        modality_ratio = text_strength / (vision_strength + 1e-08)
        modality_ratio = jnp.broadcast_to(modality_ratio, (b, s, 1))
        router_input = jnp.concatenate([h, modality_ratio], axis=-1)
        gate_logits = router_input @ gate_w + gate_b
        gate_scores = jax.nn.softmax(gate_logits, axis=-1)
        top_val, top_idx = jax.lax.top_k(gate_scores, TOP_K)
        top_val = top_val / (jnp.sum(top_val, axis=-1, keepdims=True) + 1e-08)
        expert_out = _expert_outputs(h, w1, b1, w2, b2)
        moe_out = jnp.zeros_like(h)
        batch_idx = jnp.arange(b)
        for i in range(TOP_K):
            j = top_idx[:, 0, i]
            out_i = expert_out[j, batch_idx]
            moe_out = moe_out + top_val[..., i:i + 1] * out_i
        return moe_out
    x = x + _L0_ffn_ref(_L0_cond_ref(x, cond_128, L0_cond_weight, L0_cond_c_weight, fside_S_0), L0_ffn_base_W, L0_ffn_gate_W, L0_ffn_lora_A, L0_ffn_lora_B)
    x = x + _L1_ffn_ref(_L1_cond_ref(x, cond_128, L1_cond_W0, L1_cond_b0, L1_cond_W1, L1_cond_b1, L1_cond_W2, L1_cond_b2, L1_cond_weight, L1_cond_bias_k), L1_ffn_w, L1_ffn_b)
    x = x + _L2_ffn_ref(_L2_cond_ref(x, cond_128, L2_cond_W0, L2_cond_b0, L2_cond_W1, L2_cond_b1, L2_cond_W2, L2_cond_b2, L2_cond_weight, L2_cond_bias_k), L2_ffn_W_gate, L2_ffn_W_up, L2_ffn_W_down)
    x = x + _L3_ffn_ref(_L3_cond_ref(x, cond_128, L3_cond_W0, L3_cond_b0, L3_cond_W1, L3_cond_b1, L3_cond_W2, L3_cond_b2, L3_cond_weight, L3_cond_bias_k), L3_ffn_gate_w, L3_ffn_gate_b, L3_ffn_w1, L3_ffn_b1, L3_ffn_w2, L3_ffn_b2)
    return x

_drawn_inputs = setup_inputs


def setup_inputs(seed=0):
    import zlib

    import numpy as np

    out = dict(_drawn_inputs(seed))
    spreads = {'L1_cond_b0': (0.0, 0.8),
     'L1_cond_b1': (0.0, 0.776),
     'L1_cond_b2': (0.0, 0.462),
     'L2_cond_b0': (0.0, 0.1),
     'L2_cond_b1': (0.0, 0.1),
     'L2_cond_b2': (0.0, 0.1),
     'L3_cond_b0': (0.0, 0.545),
     'L3_cond_b1': (0.0, 0.559),
     'L3_cond_b2': (0.0, 0.8),
     'L3_ffn_gate_b': (0.0, 2.0),
     'L3_ffn_b1': (0.0, 2.0),
     'L3_ffn_b2': (0.0, 2.0)}
    factors = {'L1_cond_bias_k': 37.508,
     'L1_ffn_b': 44.988,
     'L2_cond_bias_k': 5.483,
     'L3_cond_bias_k': 55.608}
    for name, (base, spread) in spreads.items():
        noise = np.random.default_rng([zlib.crc32(name.encode()), seed]).standard_normal(out[name].shape)
        drawn = base * np.exp(spread * noise) if base else spread * noise
        out[name] = jnp.asarray(drawn.astype(out[name].dtype))
    for name, factor in factors.items():
        out[name] = (out[name] * factor).astype(out[name].dtype)
    return out
```

```python
from contextlib import ExitStack

import concourse.bass as bass
from concourse import mybir

F32 = mybir.dt.float32
F32R = mybir.dt.float32r
BF16 = mybir.dt.bfloat16
U32 = mybir.dt.uint32
ALU = mybir.AluOpType
ACT = mybir.ActivationFunctionType
AX = mybir.AxisListType

P = 128
BATCH, CH, D = 64, 32, 512
BPT = P // CH
TILES = BATCH // BPT
GT = 4
GROUPS = TILES // GT
GTOK = GT * P
KT = D // P
TAPS, CONV_GROUPS = 9, 4
PH = 4
SHIFTS = 3
MW = P + SHIFTS - 1
E0, RANK = 28, 8
ER = E0 * RANK
HB = ER // 2
LORA_SCALE = 2.0
MIX = 8
HID = 128
COND_LAYERS = 3
AGW = CH * CH
AGB = AGW + CH
QMAX, QEPS = 127.0, 1e-8
MAGIC = 1.5 * 2.0 ** 23
M2 = 1792
MT = M2 // P
E3 = 3
FT = D // P
F3 = E3 * FT
VIS = int(CH * 0.3)
LAG2, LAG3 = 2, 4
HSLOTS = 3


class Chain:

    def __init__(self, eng, sem):
        self.eng, self.sem, self.base, self.k = eng, sem, 0, 0

    def begin(self, base):
        self.base, self.k = base, 0

    def link(self, ins):
        self.k += 1
        ins.then_inc(self.sem, 1)
        self.eng.wait_ge(self.sem, self.base + self.k)


def parts(a, b):
    (ah, al), (bh, bl) = a, b
    return ((ah, bh), (ah, bl), (al, bh))


def build(nc, x_rows, x_taps, cond_t, fside, cw_t, conv_w, l0_w, l0_ga, l0_lb,
          mlp_w01, mlp_w2, mlp_b01, mlp_b2, mix_w, mix_b, l1_w, l1_b,
          wg, wu, wd, gate_w, gate_w_last, gate_b, w1, b1, w2, b2, out):
    with ExitStack() as ctx:
        def sb(name, shape, dt, stack=ctx):
            return stack.enter_context(nc.sbuf_tensor(name, shape, dt))

        def sem(name):
            return ctx.enter_context(nc.semaphore(name))

        xd = nc.dram_tensor("xd", [2 * TILES, P, D], F32, kind="Internal").ap()
        aggd = nc.dram_tensor("aggd", [COND_LAYERS * BATCH, AGB], F32, kind="Internal").ap()
        ctxd = nc.dram_tensor("ctxd", [BATCH * CH], F32, kind="Internal").ap()
        swd = nc.dram_tensor("swd", [KT, P], F32, kind="Internal").ap()

        xc = sb("xc", [P, 2, D], F32)
        xres = sb("xres", [P, GT, D], F32)
        ag1 = sb("ag1", [P, TILES, CH], F32)
        ag23 = sb("ag23", [P, 2 * TILES, CH], F32)
        bcol1 = sb("bcol1", [P, TILES], F32)
        bias0 = sb("bias0", [P, 2, P], F32)
        bias23 = sb("bias23", [P, GTOK], F32)
        bdf = sb("bdf", [P, GT, P], F32)
        bdh = sb("bdh", [P, GT, P], F32R)
        bdl = sb("bdl", [P, GT, P], F32R)
        mask4 = sb("mask4", [P, BPT], F32)
        ident = sb("ident", [P, P], F32)
        identr = sb("identr", [P, P], F32R)
        identb = sb("identb", [P, P], BF16)
        ones = sb("ones", [P, P], F32)
        first = sb("first", [P, P], F32)
        sel = sb("sel", [E3, E3, P], F32)
        selr = sb("selr", [E3, E3, P], F32R)
        iota = sb("iota", [P, E0], F32)
        gwh = sb("gwh", [P, KT, E3], F32R)
        gwl = sb("gwl", [P, KT, E3], F32R)
        gwb = sb("gwb", [P, E3], F32)
        gbb = sb("gbb", [P, E3], F32)
        b1c = sb("b1c", [P, F3], F32)
        b2h = sb("b2h", [E3, D], F32R)
        b2l = sb("b2l", [E3, D], F32R)
        sx = sb("sx", [P, 4], F32)

        with ExitStack() as st:
            conv_raw = sb("conv_raw", [P, SHIFTS, P], F32, st)
            ga_raw = sb("ga_raw", [P, KT, ER + E0], F32, st)
            w0_raw = sb("w0_raw", [P, KT, D], F32, st)
            lb_raw = sb("lb_raw", [HB, 2, D], F32, st)
            w1_raw = sb("w1_raw", [P, KT, D], F32, st)
            wq_rows = sb("wq_rows", [P, KT, D], BF16, st)
            gw_raw = sb("gw_raw", [P, KT, E3], F32, st)
            b2_raw = sb("b2_raw", [E3, D], F32, st)
            condt = sb("condt", [P, BATCH], F32, st)
            cwt = sb("cwt", [P, CH], F32, st)
            fsb = sb("fsb", [BATCH, CH], F32, st)
            mw01 = sb("mw01", [P, COND_LAYERS, 2, HID], F32, st)
            mw2 = sb("mw2", [P, COND_LAYERS, MIX], F32, st)
            mb01 = sb("mb01", [P, COND_LAYERS, 2], F32, st)
            mb2 = sb("mb2", [BATCH, COND_LAYERS, MIX], F32, st)
            mixw = sb("mixw", [MIX, COND_LAYERS, AGW], F32, st)
            mixb = sb("mixb", [MIX, COND_LAYERS, CH], F32, st)
            hid1 = sb("hid1", [P, COND_LAYERS, BATCH], F32, st)
            hid2 = sb("hid2", [P, COND_LAYERS, BATCH], F32, st)
            att = sb("att", [BATCH, COND_LAYERS, MIX], F32, st)
            atte = sb("atte", [BATCH, COND_LAYERS, MIX], F32, st)
            attm = sb("attm", [BATCH, 3, COND_LAYERS], F32, st)
            attt = sb("attt", [MIX, COND_LAYERS, BATCH], F32, st)
            aggs = sb("aggs", [BATCH, 2, AGB], F32, st)
            ctxs = sb("ctxs", [BATCH, CH], F32, st)
            wsc = sb("wsc", [P, 3, KT], F32, st)
        with ExitStack() as st:
            w2h = sb("w2h", [P, E3, FT, D], F32R, st)
            w2l = sb("w2l", [P, E3, FT, D], F32R, st)
        wgr = sb("wgr", [P, KT, M2], F32R)
        wur = sb("wur", [P, KT, M2], F32R)

        with ExitStack() as st:
            w1bh = sb("w1bh", [P, KT, D], F32R, st)
            w1bl = sb("w1bl", [P, KT, D], F32R, st)
            gbc = sb("gbc", [P, E3, GTOK], F32, st)
            ltf = sb("ltf", [E3, GTOK], F32, st)
            gth = sb("gth", [E3, GTOK], F32R, st)
            gtl = sb("gtl", [E3, GTOK], F32R, st)
            rs = sb("rs", [P, 2, KT, GT * BPT], F32, st)
            rt = sb("rt", [P, 240], F32, st)
        wdr = sb("wdr", [P, MT, D], F32R)
        sb("rest3", [P, 384], F32)
        with ExitStack() as st:
            cvh = sb("cvh", [P, SHIFTS, P], F32R, st)
            cvl = sb("cvl", [P, SHIFTS, P], F32R, st)
            gah = sb("gah", [P, KT, ER + E0], F32R, st)
            gal = sb("gal", [P, KT, ER + E0], F32R, st)
            w0h = sb("w0h", [P, KT, D], F32R, st)
            w0l = sb("w0l", [P, KT, D], F32R, st)
            lbh = sb("lbh", [HB, 2, D], F32R, st)
            lbl = sb("lbl", [HB, 2, D], F32R, st)
            wq = sb("wq", [P, KT, D], BF16, st)
            swb = sb("swb", [P, D], F32, st)
            b1b = sb("b1b", [P, D], F32, st)
            tap = sb("tap", [P, 2, BPT, MW], F32, st)
            taph = sb("taph", [P, BPT, MW], F32R, st)
            tapl = sb("tapl", [P, BPT, MW], F32R, st)
            t0f = sb("t0f", [P, PH, P], F32, st)
            t0h = sb("t0h", [P, PH, P], F32R, st)
            t0l = sb("t0l", [P, PH, P], F32R, st)
            xin = sb("xin", [P, 2, D], F32, st)
            lg = sb("lg", [P, E0], F32, st)
            mx8 = sb("mx8", [P, 8], F32, st)
            ix8 = sb("ix8", [P, 8], U32, st)
            gs = sb("gs", [P, 8], F32, st)
            g0 = sb("g0", [P, 3, E0], F32, st)
            hm = sb("hm", [P, ER], F32, st)
            hmh = sb("hmh", [P, ER], F32R, st)
            hml = sb("hml", [P, ER], F32R, st)
            hts = sb("hts", [HB, 2, 2, P], F32R, st)
            x1 = sb("x1", [P, D], F32, st)
            x1h = sb("x1h", [P, D], F32R, st)
            x1l = sb("x1l", [P, D], F32R, st)
            x1b = sb("x1b", [P, D], F32, st)
            c1 = sb("c1", [P, D], F32, st)
            qb = sb("qb", [P, D], BF16, st)
            qt = sb("qt", [P, KT, P], BF16, st)
            yt = sb("yt", [P, D], F32, st)
            xo = sb("xo", [P, 2, D], F32, st)
        xch = sb("xch", [P, 2, D], F32R)
        xcl = sb("xcl", [P, 2, D], F32R)
        tf = sb("tf", [P, KT, GTOK], F32)
        th = sb("th", [P, KT, GTOK], F32R)
        tl = sb("tl", [P, KT, GTOK], F32R)
        hh = sb("hh", [P, HSLOTS, GTOK], F32R)
        hl = sb("hl", [P, HSLOTS, GTOK], F32R)
        sil = sb("sil", [P, 2, GTOK], F32)
        hf = sil
        raw3 = sb("raw3", [P, KT // 2, D], F32)
        w1ah = sb("w1ah", [P, 2, KT, D], F32R)
        w1al = sb("w1al", [P, 2, KT, D], F32R)

        bank = [ctx.enter_context(nc.psum_tensor(f"bank{i}", [P, 512], F32)) for i in range(8)]
        p_cv, p_ga, p_ht, p_y0, p_c1, p_qt, p_y1 = bank[:7]
        p_acc, p_pre = bank[4:8], bank[0:4]

        d_cond, d_mlp, d_mix, d_conv, d_ga, d_w0, d_lb, d_w1, d_l3 = (
            sem(f"d_{n}") for n in "cond mlp mix conv ga w0 lb w1 l3".split())
        d_sw, d_swb, d_ctx, d_agg, d_tab, d_b1b = (sem(f"d_{n}") for n in "sw swb ctx agg tab b1b".split())
        s_const = sem("s_const")
        s_constv = sem("s_constv")
        s_cvs, s_gas, s_w0s, s_lbs, s_l3s = (sem(f"s_{n}") for n in "cvs gas w0s lbs l3s".split())
        s_ctx, s_ctxs, s_m1, s_g1, s_m2, s_g2, s_m3, s_lm, s_ex, s_at, s_att, s_atc, s_ag, s_agc = (
            sem(f"s_{n}") for n in "ctx ctxs m1 g1 m2 g2 m3 lm ex at att atc ag agc".split())
        s_sw, s_wqr, s_wqt, s_wqc = (sem(f"s_{n}") for n in "sw wqr wqt wqc".split())
        ch_set = sem("ch_set")
        d_tap, d_xin, d_b0, d_st1 = ([sem(f"d_{n}{i}") for i in range(2)] for n in "tap xin b0 st1_".split())
        (s_taph, s_tapl, s_cv, s_t0f, s_t0h, s_t0l, s_ga, s_gd, s_ge, s_hm, s_hmh, s_hml, s_base, s_ht, s_htc,
         s_y0, s_x1, s_x1h, s_x1l, s_x1b, s_bdf, s_bdh, s_bdl, s_cd1, s_c1, s_qb, s_qt, s_qtc, s_y1, s_x2) = (
            sem(f"s1_{n}") for n in ("taph tapl cv t0f t0h t0l ga gd ge hm hmh hml base ht htc "
                                     "y0 x1 x1h x1l x1b bdf bdh bdl cd1 c1 qb qt qtc y1 x2").split())
        ch_gate, ch_q = sem("ch_gate"), sem("ch_q")
        d_xc = [sem(f"d_xc{i}") for i in range(2)]
        d_bias, d_xres, d_st = sem("d_bias"), sem("d_xres"), sem("d_st")
        s_xch, s_xclp, s_xcld, s_gf, s_gh, s_gl, s_cond, s_tf, s_th, s_tld, s_tlp, s_res = (
            sem(f"s2_{n}") for n in "xch xclp xcld gf gh gl cond tf th tld tlp res".split())
        d_wg, d_wd, d_raw = sem("d_wg"), sem("d_wd"), sem("d_raw")
        s_w3 = sem("s_w3")
        s_gate, s_up, s_sil, s_hf, s_hh, s_hl, s_down = (sem(f"s2_{n}") for n in "gate up sil hf hh hl down".split())
        (s_lg, s_ltf, s_lgt, s_lgc, s_rs, s_stat, s_dd, s_ee, s_g, s_gt, s_gth, s_gtl, s_gb, s_gbc) = (
            sem(f"s3_{n}") for n in "lg ltf lgt lgc rs stat dd ee g gt gth gtl gb gbc".split())
        s_pre, s_act, s_hf3, s_hh3, s_hl3, s_down3 = (sem(f"s3_{n}") for n in "pre act hf hh hl down".split())
        ch_rt = sem("ch_rt")

        block = ctx.enter_context(nc.Block())

        @block.sync
        def _(sp):
            sp.dma_start(condt[:], cond_t).then_inc(d_cond, 16)
            sp.dma_start(cwt[:], cw_t).then_inc(d_cond, 16)
            sp.dma_start(fsb[:], fside.partition_broadcast(BATCH)).then_inc(d_cond, 16)
            sp.dma_start(tap[:, 0], x_taps[:, 0:BPT, :]).then_inc(d_tap[0], 16)
            sp.dma_start(conv_raw[:], conv_w).then_inc(d_conv, 16)
            sp.dma_start(tap[:, 1], x_taps[:, BPT:2 * BPT, :]).then_inc(d_tap[1], 16)
            sp.dma_start(ga_raw[:], l0_ga).then_inc(d_ga, 16)
            sp.dma_start(w0_raw[:], l0_w).then_inc(d_w0, 16)
            sp.dma_start(lb_raw[:], l0_lb).then_inc(d_lb, 16)
            sp.dma_start(xin[:, 0], x_rows[0]).then_inc(d_xin[0], 16)
            sp.wait_ge(s_ctxs, 1)
            sp.dma_start(ctxd.rearrange("(b c) -> b c", c=CH), ctxs[:]).then_inc(d_ctx, 16)
            sp.wait_ge(d_ctx, 16)
            sp.dma_start(bias0[:, 0], ctxd[0:P].partition_broadcast(P)).then_inc(d_b0[0], 16)
            sp.wait_ge(s_sw, 1)
            sp.dma_start(swd.rearrange("k p -> p k"), wsc[:, 1, :], allow_slow_non_contiguous=True).then_inc(d_sw, 16)
            sp.wait_ge(d_sw, 16)
            sp.dma_start(swb[:], swd.rearrange("k p -> (k p)").partition_broadcast(P)).then_inc(d_swb, 16)
            for l in range(COND_LAYERS):
                sp.wait_ge(s_agc, 3 * (l + 1))
                sp.dma_start(aggd[l * BATCH:(l + 1) * BATCH, :], aggs[:, l % 2]).then_inc(d_agg, 16)
                sp.wait_ge(d_agg, 16 * (l + 1))
                mixed = aggd[l * BATCH:(l + 1) * BATCH, :].rearrange("(t b) n -> b t n", b=BPT)
                for b in range(BPT):
                    rows = slice(CH * b, CH * (b + 1))
                    dst = ag1[rows] if l == 0 else ag23[rows, (l - 1) * TILES:l * TILES]
                    sp.dma_start(dst, mixed[b, :, 0:AGW].rearrange("t (i o) -> i t o", i=CH)).then_inc(d_tab, 16)
                    if l == 0:
                        sp.dma_start(bcol1[rows], mixed[b, :, AGW:AGB].rearrange("t o -> o t"),
                                     allow_slow_non_contiguous=True).then_inc(d_tab, 16)

            def step(t, p, load=True, tail=True):
                if load:
                    n = sp.snap((t + 2) * BPT)
                    sp.wait_ge(s_tapl, t + 1)
                    sp.dma_start(tap[:, p], x_taps[:, bass.ds(n, BPT), :]).then_inc(d_tap[p], 16)
                if tail:
                    if not (isinstance(t, int) and t == 0):
                        sp.wait_ge(s_t0f, t)
                        sp.wait_ge(s_x1, t)
                    sp.dma_start(bias0[:, 1 - p], ctxd[bass.ds((t + 1) * P, P)].partition_broadcast(P)).then_inc(d_b0[1 - p], 16)
                    sp.dma_start(xin[:, 1 - p], x_rows[bass.ds(t + 1, 1)].rearrange("a p d -> (a p) d")).then_inc(d_xin[1 - p], 16)
                if not (isinstance(t, int) and t == 0):
                    sp.wait_ge(s_x2, t)
                    sp.dma_start(xd[bass.ds(t - 1, 1)].rearrange("a p d -> (a p) d"), xo[:, 1 - p]).then_inc(d_st1[1 - p], 16)

            step(0, 0)
            step(1, 1)
            step(2, 0)
            with sp.Fori(1, 6) as i:
                step(i * 2 + 1, 1)
                step(i * 2 + 2, 0)
            step(13, 1)
            step(14, 0, load=False)
            step(15, 1, load=False, tail=False)
            step(16, 0, load=False, tail=False)

            def load_xc(row, j):
                sp.dma_start(xc[:, j % 2], xd[bass.ds(row + j, 1)].rearrange("a p d -> (a p) d")).then_inc(d_xc[j % 2], 16)

            def load_bias(c):
                sp.dma_start(bias23[:].rearrange("p (b o) -> p b o", o=CH),
                             aggd[bass.ds(c * (GT * BPT) + BATCH, GT * BPT), AGW:AGB].partition_broadcast(P)).then_inc(d_bias, 16)

            for p in range(2):
                sp.wait_ge(d_st1[p], 16 * TILES // 2)
            load_xc(0, 0)
            load_xc(0, 1)
            load_bias(0)
            sp.wait_ge(s_xch, 2)
            sp.wait_ge(s_xclp, 2)
            load_xc(0, 2)
            load_xc(0, 3)

            def load_next(c):
                row = sp.snap(c * GT)
                sp.wait_ge(s_tf, c * KT)
                load_bias(c)
                sp.wait_ge(s_xcld, c * 2)
                load_xc(row, 0)
                load_xc(row, 1)
                sp.wait_ge(s_xclp, c * 2 + 2)
                load_xc(row, 2)
                load_xc(row, 3)

            def load_xres(c):
                sp.dma_start(xres[:], xd[bass.ds(c * GT, GT)].rearrange("a p d -> p a d")).then_inc(d_xres, 16)

            load_xres(0)

            def group(c, r, dst, ahead=True):
                if ahead:
                    load_next(c + 1)
                sp.wait_ge(s_res, (c + 1) * GT)
                sp.dma_start(dst[bass.ds(r * GT, GT)].rearrange("a p d -> p a d"), xres[:]).then_inc(d_st, 16)
                if ahead:
                    sp.wait_ge(d_st, (c + 1) * 16)
                    load_xres(c + 1)

            with sp.Fori(0, GROUPS) as s:
                group(s, s + GROUPS, xd)
            with sp.Fori(0, GROUPS - 1) as r:
                group(r + GROUPS, r, out)
            group(2 * GROUPS - 1, GROUPS - 1, out, ahead=False)
            sp.wait_ge(d_st, 16 * 2 * GROUPS)

        @block.gpsimd
        def _(pool):
            nc.gpsimd.memset(ident[:], 0.0).then_inc(s_const, 1)
            nc.gpsimd.memset(mask4[:], 1.0).then_inc(s_const, 1)
            nc.gpsimd.memset(first[:], 0.0).then_inc(s_const, 1)
            nc.gpsimd.memset(sel[:], 0.0).then_inc(s_const, 1)
            nc.gpsimd.memset(ones[:], 1.0).then_inc(s_const, 1)
            nc.gpsimd.iota(iota[:], [[1, E0]], base=0, channel_multiplier=0,
                           allow_small_or_imprecise_dtypes=True).then_inc(s_const, 1)
            pool.wait_ge(s_const, 6)
            nc.gpsimd.affine_select(out=ident[:], in_=ident[:], compare_op=ALU.not_equal, fill=1.0, base=0,
                                    pattern=[[-1, P]], channel_multiplier=1).then_inc(s_const, 1)
            nc.gpsimd.affine_select(out=mask4[:], in_=mask4[:], compare_op=ALU.is_ge, fill=0.0, base=0,
                                    pattern=[[-CH, BPT]], channel_multiplier=1).then_inc(s_const, 1)
            nc.gpsimd.affine_select(out=first[:].rearrange("p (b c) -> p b c", c=CH),
                                    in_=first[:].rearrange("p (b c) -> p b c", c=CH), compare_op=ALU.not_equal,
                                    fill=1.0, base=0, pattern=[[-CH, BPT], [0, CH]], channel_multiplier=1).then_inc(s_const, 1)
            nc.gpsimd.affine_select(out=sel[:], in_=sel[:], compare_op=ALU.not_equal, fill=1.0, base=0,
                                    pattern=[[-1, E3], [0, P]], channel_multiplier=1).then_inc(s_const, 1)
            pool.wait_ge(s_const, 10)
            nc.gpsimd.affine_select(out=mask4[:], in_=mask4[:], compare_op=ALU.is_ge, fill=0.0, base=CH - 1,
                                    pattern=[[CH, BPT]], channel_multiplier=-1).then_inc(s_const, 1)
            pool.wait_ge(s_const, 11)

            def block_diag(dst, table):
                for n in range(dst.shape[1]):
                    ins = nc.gpsimd.tensor_tensor(
                        dst[:, n].rearrange("p (b o) -> p b o", b=BPT),
                        table[:, n:n + 1, :].to_broadcast([P, BPT, CH]),
                        mask4[:].unsqueeze(2).to_broadcast([P, BPT, CH]), ALU.mult)
                return ins

            def tap_lo(t, p):
                pool.wait_ge(s_taph, t + 1)
                nc.gpsimd.tensor_tensor(tapl[:], tap[:, p], taph[:].bitcast(F32), ALU.subtract).then_inc(s_tapl, 1)

            def diag_tile(t, p):
                if not (isinstance(t, int) and t < 2):
                    pool.wait_ge(s_cd1, t - 1)
                block_diag(bdf[:, p:p + 1], ag1[:, bass.ds(t, 1)]).then_inc(s_bdf, 1)
                pool.wait_ge(s_bdh, t + 1)
                nc.gpsimd.tensor_tensor(bdl[:, p], bdf[:, p], bdh[:, p].bitcast(F32), ALU.subtract).then_inc(s_bdl, 1)

            def step(t, p, conv=True, tile=True):
                later = not (isinstance(t, int) and t == 0)
                if later:
                    pool.wait_ge(s_x1h, t)
                    nc.gpsimd.tensor_tensor(x1l[:], x1[:], x1h[:].bitcast(F32), ALU.subtract).then_inc(s_x1l, 1)
                    if not (isinstance(t, int) and t == 1):
                        pool.wait_ge(s_x2, t - 1)
                    nc.gpsimd.tensor_tensor(x1b[:], x1[:], b1b[:], ALU.add).then_inc(s_x1b, 1)
                if tile:
                    diag_tile(t, p)
                if conv:
                    tap_lo(t + 2, p)

            tap_lo(0, 0)
            tap_lo(1, 1)
            pool.wait_ge(d_tab, 16 * 2 * BPT)
            pool.wait_ge(d_b1b, 16)
            step(0, 0)
            pool.wait_ge(d_agg, 16 * COND_LAYERS)
            pool.wait_ge(s_wqt, 4)
            pool.wait_ge(s_l3s, 4)
            pool.wait_ge(s_lbs, 2)
            pool.dma_start(wdr[:], wd).then_inc(d_wd, 16)
            pool.dma_start(wgr[:], wg).then_inc(d_wg, 16)
            pool.dma_start(wur[:], wu).then_inc(d_wg, 16)
            step(1, 1)
            step(2, 0)
            with pool.Fori(1, 6) as i:
                step(i * 2 + 1, 1)
                step(i * 2 + 2, 0)
            step(13, 1)
            step(14, 0, conv=False)
            step(15, 1, conv=False)
            step(16, 0, conv=False, tile=False)

            def diag_group(c, first_=False):
                if not first_:
                    pool.wait_ge(s_cond, c * GT)
                block_diag(bdf[:], ag23[:, bass.ds(c * GT, GT)]).then_inc(s_gf, 1)
                pool.wait_ge(s_gh, c + 1)
                nc.gpsimd.tensor_tensor(bdl[:], bdf[:], bdh[:].bitcast(F32), ALU.subtract).then_inc(s_gl, 1)

            def x_lo(c, j):
                pool.wait_ge(s_xch, c * GT + j + 1)
                nc.gpsimd.tensor_tensor(xcl[:, j % 2], xc[:, j % 2], xch[:, j % 2].bitcast(F32), ALU.subtract).then_inc(s_xclp, 1)

            def t_lo(c):
                for kt in (1, 3):
                    pool.wait_ge(s_th, c * KT + kt + 1)
                    nc.gpsimd.tensor_tensor(tl[:, kt], tf[:, kt], th[:, kt].bitcast(F32), ALU.subtract).then_inc(s_tlp, 1)

            def split3(n, hi, lo, src):
                for half in range(2):
                    done = 8 * n + 4 * half
                    if done:
                        pool.wait_ge(s_w3, done)
                    pool.dma_start(raw3[:], src[:, 2 * half:2 * half + 2]).then_inc(d_raw, 16)
                    pool.wait_ge(d_raw, 16 * (2 * n + half + 1))
                    for k in range(2):
                        nc.gpsimd.tensor_scalar(hi[:, 2 * half + k], raw3[:, k], 1.0, 1.0, ALU.mult, ALU.mult).then_inc(s_w3, 1)
                    for k in range(2):
                        pool.wait_ge(s_w3, done + k + 1)
                        nc.gpsimd.tensor_tensor(lo[:, 2 * half + k], raw3[:, k], hi[:, 2 * half + k].bitcast(F32),
                                                ALU.subtract).then_inc(s_w3, 1)

            pool.wait_ge(d_tab, 16 * 4 * BPT)
            pool.wait_ge(s_x2, TILES)
            diag_group(0, True)
            x_lo(0, 0)
            x_lo(0, 1)
            t_lo(0)
            split3(0, w1ah[:, 0], w1al[:, 0], w1[:, 0])
            split3(1, w1ah[:, 1], w1al[:, 1], w1[:, 1])

            def ahead(c):
                diag_group(c)
                x_lo(c, 0)
                x_lo(c, 1)
                t_lo(c)

            with pool.Fori(0, GROUPS) as s:
                ahead(s + 1)
            pool.wait_ge(s_up, MT * GROUPS)
            split3(2, w2h[:, 0], w2l[:, 0], w2[:, 0])
            pool.wait_ge(s_down, MT * GROUPS)
            split3(3, w1bh[:], w1bl[:], w1[:, 2])
            split3(4, w2h[:, 1], w2l[:, 1], w2[:, 1])
            split3(5, w2h[:, 2], w2l[:, 2], w2[:, 2])
            with pool.Fori(0, GROUPS - 1) as r:
                ahead(r + GROUPS + 1)

        @block.scalar
        def _(act):
            act.dma_start(mw01[:], mlp_w01).then_inc(d_mlp, 16)
            act.dma_start(mw2[:], mlp_w2).then_inc(d_mlp, 16)
            act.dma_start(mb01[:], mlp_b01).then_inc(d_mlp, 16)
            act.dma_start(mb2[:], mlp_b2.partition_broadcast(BATCH)).then_inc(d_mlp, 16)
            act.dma_start(mixw[:], mix_w).then_inc(d_mix, 16)
            act.dma_start(mixb[:], mix_b).then_inc(d_mix, 16)
            act.dma_start(w1_raw[:], l1_w).then_inc(d_w1, 16)
            act.dma_start(b1b[:], l1_b.partition_broadcast(P)).then_inc(d_b1b, 16)
            act.dma_start(gw_raw[:], gate_w).then_inc(d_l3, 16)
            act.dma_start(b2_raw[:], b2).then_inc(d_l3, 16)
            act.dma_start(gwb[:], gate_w_last.partition_broadcast(P)).then_inc(d_l3, 16)
            act.dma_start(gbb[:], gate_b.partition_broadcast(P)).then_inc(d_l3, 16)
            act.dma_start(b1c[:], b1).then_inc(d_l3, 16)

            def tap_hi(t, p, n):
                act.wait_ge(d_tap[p], n * 16)
                if not (isinstance(t, int) and t == 0):
                    act.wait_ge(s_cv, t)
                nc.scalar.activation(taph[:], tap[:, p], ACT.Copy).then_inc(s_taph, 1)

            tap_hi(0, 0, 1)
            act.wait_ge(d_conv, 16)
            nc.scalar.activation(cvh[:], conv_raw[:], ACT.Copy).then_inc(s_cvs, 1)
            act.wait_ge(s_const, 11)
            nc.scalar.activation(identr[:], ident[:], ACT.Copy).then_inc(s_constv, 1)
            nc.scalar.activation(identb[:], ident[:], ACT.Copy).then_inc(s_constv, 1)
            nc.scalar.activation(selr[:], sel[:], ACT.Copy).then_inc(s_constv, 1)
            act.wait_ge(d_mlp, 64)
            act.wait_ge(s_m1, COND_LAYERS)
            for l in range(COND_LAYERS):
                nc.scalar.activation(hid1[:, l], bank[0][:, l * BATCH:(l + 1) * BATCH], ACT.Gelu,
                                     bias=mb01[:, l, 0:1]).then_inc(s_g1, 1)
            act.wait_ge(s_m2, COND_LAYERS)
            for l in range(COND_LAYERS):
                nc.scalar.activation(hid2[:, l], bank[1][:, l * BATCH:(l + 1) * BATCH], ACT.Gelu,
                                     bias=mb01[:, l, 1:2]).then_inc(s_g2, 1)
            act.wait_ge(s_lm, 1)
            nc.scalar.activation(atte[:], att[:], ACT.Exp).then_inc(s_ex, 1)
            act.wait_ge(d_ga, 16)
            nc.scalar.activation(gah[:], ga_raw[:], ACT.Copy).then_inc(s_gas, 1)
            act.wait_ge(d_w0, 16)
            nc.scalar.activation(w0h[:], w0_raw[:], ACT.Copy).then_inc(s_w0s, 1)
            act.wait_ge(d_lb, 16)
            nc.scalar.activation(lbh[:], lb_raw[:], ACT.Copy).then_inc(s_lbs, 1)
            act.wait_ge(d_l3, 80)
            nc.scalar.activation(gwh[:], gw_raw[:], ACT.Copy).then_inc(s_l3s, 1)
            nc.scalar.activation(b2h[:], b2_raw[:], ACT.Copy).then_inc(s_l3s, 1)
            tap_hi(1, 1, 1)

            def t0_hi(t):
                act.wait_ge(s_t0f, t + 1)
                if not (isinstance(t, int) and t == 0):
                    act.wait_ge(s_base, t)
                nc.scalar.activation(t0h[:], t0f[:], ACT.Copy).then_inc(s_t0h, 1)

            t0_hi(0)

            def step(t, p, k, tap_=True, conv=True, tile=True):
                later = not (isinstance(t, int) and t == 0)
                later2 = not (isinstance(t, int) and t <= 1)
                if later:
                    act.wait_ge(s_x1, t)
                    if later2:
                        act.wait_ge(s_cd1, t - 1)
                    nc.scalar.activation(x1h[:], x1[:], ACT.Copy).then_inc(s_x1h, 1)
                if tile:
                    act.wait_ge(s_gd, t + 1)
                    nc.scalar.activation(gs[:, 4:5], gs[:, 3:4], ACT.Exp).then_inc(s_ge, 1)
                    act.wait_ge(s_hm, t + 1)
                    if later:
                        act.wait_ge(s_ht, t)
                    nc.scalar.activation(hmh[:], hm[:], ACT.Copy).then_inc(s_hmh, 1)
                if later:
                    act.wait_ge(s_cd1, t)
                    if later2:
                        act.wait_ge(s_qb, t - 1)
                    act.wait_ge(d_tab, 16 * 2 * BPT)
                    nc.scalar.activation(c1[:], p_c1[:], ACT.Identity, bias=bcol1[:, bass.ds(t - 1, 1)]).then_inc(s_c1, 1)
                if tile:
                    act.wait_ge(s_bdf, t + 1)
                    nc.scalar.activation(bdh[:, p], bdf[:, p], ACT.Copy).then_inc(s_bdh, 1)
                if tap_:
                    tap_hi(t + 2, p, k + 1)
                if conv:
                    t0_hi(t + 1)
                if tile:
                    act.wait_ge(s_ht, t + 1)
                    if later:
                        act.wait_ge(s_y0, t)
                    nc.scalar.activation(hts[:].rearrange("p a b n -> p (a b n)"), p_ht[0:HB, :], ACT.Copy).then_inc(s_htc, 1)
                if later:
                    act.wait_ge(s_qt, t)
                    if later2:
                        act.wait_ge(s_y1, t - 1)
                    nc.scalar.activation(qt[:].rearrange("p a n -> p (a n)"), p_qt[:].bitcast(BF16)[:, 0:D], ACT.Copy).then_inc(s_qtc, 1)

            step(0, 0, 1)
            step(1, 1, 1)
            step(2, 0, 2)
            with act.Fori(1, 6) as i:
                step(i * 2 + 1, 1, i + 1)
                step(i * 2 + 2, 0, i + 2)
            step(13, 1, 7)
            step(14, 0, 8, tap_=False)
            step(15, 1, 8, tap_=False, conv=False)
            step(16, 0, 8, tap_=False, conv=False, tile=False)

            def x_hi(c, j, k, wait_cond=True):
                act.wait_ge(d_xc[j % 2], k)
                if wait_cond:
                    act.wait_ge(s_cond, c * GT + j - 1)
                nc.scalar.activation(xch[:, j % 2], xc[:, j % 2], ACT.Copy).then_inc(s_xch, 1)

            def diag_hi(c):
                act.wait_ge(s_gf, c + 1)
                nc.scalar.activation(bdh[:], bdf[:], ACT.Copy).then_inc(s_gh, 1)

            def t_hi(c):
                for kt in range(KT):
                    act.wait_ge(s_tf, c * KT + kt + 1)
                    nc.scalar.activation(th[:, kt], tf[:, kt], ACT.Copy).then_inc(s_th, 1)

            act.wait_ge(s_x2, TILES)
            diag_hi(0)
            x_hi(0, 0, 16, False)
            x_hi(0, 1, 16, False)
            x_hi(0, 2, 32)
            x_hi(0, 3, 32)
            t_hi(0)

            def ahead(c):
                diag_hi(c)
                x_hi(c, 0, c * 32 + 16)
                x_hi(c, 1, c * 32 + 16)

            def boundary(c):
                x_hi(c, 2, c * 32 + 32)
                x_hi(c, 3, c * 32 + 32)
                t_hi(c)

            with act.Fori(0, GROUPS) as s:
                for m in range(MT):
                    act.wait_ge(s_gate, s * MT + m + 1)
                    if m >= 2:
                        act.wait_ge(s_hl, s * MT + m - 1)
                    nc.scalar.activation(sil[:, m % 2], p_pre[2 * (m % 2)][:], ACT.Silu).then_inc(s_sil, 1)
                    act.wait_ge(s_hf, s * MT + m + 1)
                    if m >= HSLOTS:
                        act.wait_ge(s_down, s * MT + m - HSLOTS + 1)
                    nc.scalar.activation(hh[:, m % HSLOTS], hf[:, m % 2], ACT.Copy).then_inc(s_hh, 1)
                    if m == 4:
                        ahead(s + 1)
                boundary(s + 1)

            def group3(r, last=False):
                act.wait_ge(s_lg, r + 1)
                nc.scalar.activation(ltf[:], p_acc[3][0:E3, :], ACT.Copy).then_inc(s_ltf, 1)
                act.wait_ge(s_dd, r + 1)
                nc.scalar.activation(rt[:, 100:108], rt[:, 92:100], ACT.Exp).then_inc(s_ee, 1)
                act.wait_ge(s_gt, r + 1)
                nc.scalar.activation(gth[:], p_acc[0][0:E3, :], ACT.Copy).then_inc(s_gth, 1)
                for f in range(F3):
                    fn = (ACT.Tanh, ACT.Gelu, ACT.Silu)[f // FT]
                    act.wait_ge(s_pre, r * F3 + f + 1)
                    if f >= 2:
                        act.wait_ge(s_hl3, r * F3 + f - 1)
                    nc.scalar.activation(sil[:, f % 2], p_pre[f % 4][:], fn, bias=b1c[:, f:f + 1]).then_inc(s_act, 1)
                    if f == 0:
                        for e in range(E3):
                            act.wait_ge(s_gb, r * E3 + e + 1)
                            nc.scalar.activation(gbc[:, e], p_acc[e + 1][:], ACT.Copy).then_inc(s_gbc, 1)
                    act.wait_ge(s_hf3, r * F3 + f + 1)
                    if f >= HSLOTS:
                        act.wait_ge(s_down3, r * F3 + f - HSLOTS + 1)
                    nc.scalar.activation(hh[:, f % HSLOTS], hf[:, f % 2], ACT.Copy).then_inc(s_hh3, 1)
                    if f == 6 and not last:
                        ahead(r + GROUPS + 1)
                if not last:
                    boundary(r + GROUPS + 1)

            with act.Fori(0, GROUPS - 1) as r:
                group3(r)
            group3(GROUPS - 1, True)

        @block.vector
        def _(dve):
            v = nc.vector
            chain = Chain(dve, ch_set)

            dve.wait_ge(s_cvs, 1)
            v.tensor_tensor(cvl[:], conv_raw[:], cvh[:].bitcast(F32), ALU.subtract).then_inc(s_cvs, 1)
            dve.wait_ge(d_cond, 48)
            dve.wait_ge(s_ctx, 1)
            v.tensor_tensor(ctxs[:], bank[2][0:BATCH, 256:256 + CH], fsb[:], ALU.add).then_inc(s_ctxs, 1)
            dve.wait_ge(d_w1, 16)
            v.tensor_reduce(wsc[:, 0, :], w1_raw[:], AX.X, ALU.max, apply_absolute_value=True).then_inc(ch_set, 1)
            dve.wait_ge(ch_set, 1)
            v.tensor_scalar(wsc[:, 1, :], wsc[:, 0, :], 1.0 / QMAX, QEPS, ALU.mult, ALU.max).then_inc(s_sw, 1)
            dve.wait_ge(s_sw, 1)
            chain.begin(1)
            chain.link(v.reciprocal(wsc[:, 2, :], wsc[:, 1, :]))
            for k in range(KT):
                chain.link(v.tensor_scalar(w1_raw[:, k], w1_raw[:, k], wsc[:, 2, k:k + 1], MAGIC, ALU.mult, ALU.add))
                v.tensor_scalar(wq_rows[:, k], w1_raw[:, k], MAGIC, QMAX, ALU.subtract, ALU.min).then_inc(s_wqr, 1)
            dve.wait_ge(s_m3, 1)
            dve.wait_ge(d_mlp, 64)
            logits = bank[2][0:BATCH, 0:COND_LAYERS * MIX].rearrange("p (l k) -> p l k", k=MIX)

            def rows(n):
                return attm[:, n, :].unsqueeze(2).to_broadcast([BATCH, COND_LAYERS, MIX])

            chain.link(v.tensor_tensor(att[:], logits, mb2[:], ALU.add))
            chain.link(v.tensor_reduce(attm[:, 0, :], att[:], AX.X, ALU.max))
            v.tensor_tensor(att[:], att[:], rows(0), ALU.subtract).then_inc(s_lm, 1)
            dve.wait_ge(s_ex, 1)
            chain.link(v.tensor_reduce(attm[:, 1, :], atte[:], AX.X, ALU.add))
            chain.link(v.reciprocal(attm[:, 2, :], attm[:, 1, :]))
            v.tensor_tensor(att[:], atte[:], rows(2), ALU.mult).then_inc(s_at, 1)
            dve.wait_ge(s_att, 1)
            v.tensor_copy(attt[:].rearrange("k l b -> k (l b)"), bank[3][0:MIX, 0:COND_LAYERS * BATCH]).then_inc(s_atc, 1)
            for l in range(COND_LAYERS):
                dve.wait_ge(s_ag, l + 1)
                if l == 2:
                    dve.wait_ge(d_agg, 16)
                lo, hi = ((4, 5), (6, 7), (4, 5))[l]
                v.tensor_copy(aggs[:, l % 2, 0:512], bank[lo][0:BATCH, :]).then_inc(s_agc, 1)
                v.tensor_copy(aggs[:, l % 2, 512:AGW], bank[hi][0:BATCH, :]).then_inc(s_agc, 1)
                v.tensor_copy(aggs[:, l % 2, AGW:AGB], bank[2][0:BATCH, l * CH:(l + 1) * CH]).then_inc(s_agc, 1)
            dve.wait_ge(s_gas, 1)
            v.tensor_tensor(gal[:], ga_raw[:], gah[:].bitcast(F32), ALU.subtract).then_inc(s_gas, 1)
            dve.wait_ge(s_w0s, 1)
            v.tensor_tensor(w0l[:], w0_raw[:], w0h[:].bitcast(F32), ALU.subtract).then_inc(s_w0s, 1)
            dve.wait_ge(s_lbs, 1)
            v.tensor_tensor(lbl[:], lb_raw[:], lbh[:].bitcast(F32), ALU.subtract).then_inc(s_lbs, 1)
            for k in range(KT):
                dve.wait_ge(s_wqt, k // 2 * 2 + 2)
                v.tensor_copy(wq[:, k], bank[7 - k // 2][:].bitcast(BF16)[:, (k % 2) * D:(k % 2 + 1) * D]).then_inc(s_wqc, 1)
            dve.wait_ge(s_l3s, 2)
            v.tensor_tensor(gwl[:], gw_raw[:], gwh[:].bitcast(F32), ALU.subtract).then_inc(s_l3s, 1)
            v.tensor_tensor(b2l[:], b2_raw[:], b2h[:].bitcast(F32), ALU.subtract).then_inc(s_l3s, 1)

            def t0_rows(t, p, n):
                dve.wait_ge(s_cv, t + 1)
                dve.wait_ge(d_b0[p], n * 16)
                v.tensor_tensor(t0f[:], p_cv[:].rearrange("p (a n) -> p a n", a=PH),
                                bias0[:, p:p + 1].to_broadcast([P, PH, P]), ALU.add).then_inc(s_t0f, 1)
                dve.wait_ge(s_t0h, t + 1)
                v.tensor_tensor(t0l[:], t0f[:], t0h[:].bitcast(F32), ALU.subtract).then_inc(s_t0l, 1)

            t0_rows(0, 0, 1)
            gate, quant = Chain(dve, ch_gate), Chain(dve, ch_q)
            GATE_LINKS, QUANT_LINKS = 9, 5

            def step(t, p, own, ahead_, stored, conv=True, tile=True):
                later = not (isinstance(t, int) and t == 0)
                later2 = not (isinstance(t, int) and t <= 1)
                if tile:
                    gate.begin(t * GATE_LINKS)
                    dve.wait_ge(s_ga, t + 1)
                    gate.link(v.tensor_copy(lg[:], p_ga[:, ER:ER + E0]))
                    v.tensor_reduce(gs[:, 2:3], lg[:], AX.X, ALU.max)
                    gate.link(v.max(mx8[:], lg[:]))
                    v.tensor_tensor(gs[:, 3:4], mx8[:, 1:2], gs[:, 2:3], ALU.subtract).then_inc(s_gd, 1)
                    gate.link(v.max_index(ix8[:], mx8[:], lg[:]))
                    gate.link(v.tensor_copy(gs[:, 0:2], ix8[:, 0:2]))
                    dve.wait_ge(s_ge, t + 1)
                    gate.link(v.tensor_scalar(gs[:, 5:6], gs[:, 4:5], 1.0, 1.0 / LORA_SCALE, ALU.add, ALU.mult))
                    gate.link(v.reciprocal(gs[:, 6:7], gs[:, 5:6]))
                    gate.link(v.tensor_tensor(gs[:, 7:8], gs[:, 4:5], gs[:, 6:7], ALU.mult))
                    v.tensor_scalar(g0[:, 0], iota[:], gs[:, 0:1], gs[:, 6:7], ALU.is_equal, ALU.mult)
                    gate.link(v.tensor_scalar(g0[:, 1], iota[:], gs[:, 1:2], gs[:, 7:8], ALU.is_equal, ALU.mult))
                    gate.link(v.tensor_tensor(g0[:, 2], g0[:, 0], g0[:, 1], ALU.add))
                    assert gate.k == GATE_LINKS
                    v.tensor_tensor(hm[:].rearrange("p (e r) -> p e r", r=RANK),
                                    p_ga[:, 0:ER].rearrange("p (e r) -> p e r", r=RANK),
                                    g0[:, 2].unsqueeze(2).to_broadcast([P, E0, RANK]), ALU.mult).then_inc(s_hm, 1)
                    dve.wait_ge(s_hmh, t + 1)
                    v.tensor_tensor(hml[:], hm[:], hmh[:].bitcast(F32), ALU.subtract).then_inc(s_hml, 1)
                if later:
                    quant.begin((t - 1) * QUANT_LINKS)
                    dve.wait_ge(s_c1, t)
                    quant.link(v.tensor_reduce(sx[:, 0:1], c1[:], AX.X, ALU.max, apply_absolute_value=True))
                    quant.link(v.tensor_scalar(sx[:, 1:2], sx[:, 0:1], 1.0 / QMAX, QEPS, ALU.mult, ALU.max))
                    quant.link(v.reciprocal(sx[:, 2:3], sx[:, 1:2]))
                    quant.link(v.tensor_scalar(c1[:], c1[:], sx[:, 2:3], MAGIC, ALU.mult, ALU.add))
                    if later2:
                        dve.wait_ge(s_qt, t - 1)
                    v.tensor_scalar(qb[:], c1[:], MAGIC, QMAX, ALU.subtract, ALU.min).then_inc(s_qb, 1)
                if conv:
                    t0_rows(t + 1, 1 - p, ahead_)
                if tile:
                    dve.wait_ge(s_y0, t + 1)
                    dve.wait_ge(d_xin[p], own * 16)
                    if later:
                        dve.wait_ge(s_x1h, t)
                        dve.wait_ge(s_x1l, t)
                        dve.wait_ge(s_x1b, t)
                    v.tensor_tensor(x1[:], p_y0[:], xin[:, p], ALU.add).then_inc(s_x1, 1)
                if later:
                    dve.wait_ge(s_y1, t)
                    dve.wait_ge(d_swb, 16)
                    quant.link(v.scalar_tensor_tensor(yt[:], p_y1[:], sx[:, 1:2], swb[:], ALU.mult, ALU.mult))
                    assert quant.k == QUANT_LINKS
                    dve.wait_ge(s_x1b, t)
                    if not (isinstance(stored, int) and stored == 0):
                        dve.wait_ge(d_st1[1 - p], stored * 16)
                    v.tensor_tensor(xo[:, 1 - p], yt[:], x1b[:], ALU.add).then_inc(s_x2, 1)

            step(0, 0, 1, 1, 0)
            step(1, 1, 1, 2, 0)
            step(2, 0, 2, 2, 0)
            with dve.Fori(1, 6) as i:
                step(i * 2 + 1, 1, i + 1, i + 2, i)
                step(i * 2 + 2, 0, i + 2, i + 2, i)
            step(13, 1, 7, 8, 6)
            step(14, 0, 8, 8, 6)
            step(15, 1, 8, None, 7, conv=False)
            step(16, 0, None, None, 7, conv=False, tile=False)

            def x_lo(c):
                for j in (2, 3):
                    dve.wait_ge(s_xch, c * GT + j + 1)
                    v.tensor_tensor(xcl[:, j % 2], xc[:, j % 2], xch[:, j % 2].bitcast(F32), ALU.subtract).then_inc(s_xcld, 1)

            def t_rows(c):
                dve.wait_ge(s_cond, (c + 1) * GT)
                dve.wait_ge(d_bias, (c + 1) * 16)

                def lo(kt):
                    dve.wait_ge(s_th, c * KT + kt + 1)
                    v.tensor_tensor(tl[:, kt], tf[:, kt], th[:, kt].bitcast(F32), ALU.subtract).then_inc(s_tld, 1)

                for kt in range(KT):
                    v.tensor_tensor(tf[:, kt], p_pre[kt][:], bias23[:], ALU.add).then_inc(s_tf, 1)
                    if kt == 1:
                        lo(0)
                lo(2)

            def residual(c, done, value):
                dve.wait_ge(done, value)
                dve.wait_ge(d_xres, (c + 1) * 16)
                for j in (3, 2, 1, 0):
                    v.tensor_tensor(xres[:, j], p_acc[j][:], xres[:, j], ALU.add).then_inc(s_res, 1)

            x_lo(0)
            t_rows(0)
            with dve.Fori(0, GROUPS) as s:
                for m in range(MT):
                    dve.wait_ge(s_up, s * MT + m + 1)
                    dve.wait_ge(s_sil, s * MT + m + 1)
                    v.tensor_tensor(hf[:, m % 2], p_pre[2 * (m % 2) + 1][:], sil[:, m % 2], ALU.mult).then_inc(s_hf, 1)
                    dve.wait_ge(s_hh, s * MT + m + 1)
                    v.tensor_tensor(hl[:, m % HSLOTS], hf[:, m % 2], hh[:, m % HSLOTS].bitcast(F32), ALU.subtract).then_inc(s_hl, 1)
                x_lo(s + 1)
                t_rows(s + 1)
                residual(s, s_down, (s + 1) * MT)

            route = Chain(dve, ch_rt)

            def col(n, w=GT):
                return rt[:, n:n + w]

            LL, RB, G, NG, I1, I3, OUT = 0, 24, 36, 48, 60, 72, 120
            DD, EE = 92, 100
            TMP = 140

            def three(n):
                return rt[:, n:n + E3 * GT].rearrange("p (e j) -> p e j", e=E3)

            def group3(r, last=False):
                tok = tf[:].rearrange("p k (b s) -> p k b s", s=CH)
                dve.wait_ge(s_tf, (r + GROUPS + 1) * KT)
                v.tensor_reduce(rs[:, 0], tok[:, :, :, 0:VIS], AX.X, ALU.add, apply_absolute_value=True).then_inc(s_rs, 1)
                v.tensor_reduce(rs[:, 1], tok[:, :, :, VIS:CH], AX.X, ALU.add, apply_absolute_value=True).then_inc(s_rs, 1)
                route.begin(r * ROUTE_LINKS)
                dve.wait_ge(s_lgt, r + 1)
                v.tensor_copy(three(LL), p_acc[2][:, 0:GT * 4].rearrange("p (j e) -> p e j", e=4)[:, 0:E3, :]).then_inc(s_lgc, 1)
                dve.wait_ge(s_stat, r + 1)
                route.link(v.tensor_tensor(rt[:, 200:232].rearrange("p (q b) -> p q b", b=BPT),
                                           p_acc[1][:, 0:32].rearrange("p (q b) -> p q b", b=BPT),
                                           mask4[:].unsqueeze(1).to_broadcast([P, 2 * GT, BPT]), ALU.mult))
                route.link(v.tensor_reduce(col(TMP, 8), rt[:, 200:232].rearrange("p (q b) -> p q b", b=BPT), AX.X, ALU.add))
                route.link(v.tensor_scalar(col(TMP + 8), col(TMP), 1.0 / (VIS * D), 1e-8, ALU.mult, ALU.add))
                route.link(v.reciprocal(col(TMP + 12), col(TMP + 8)))
                route.link(v.scalar_tensor_tensor(col(TMP + 16), col(TMP + 4), 1.0 / ((CH - VIS) * D), col(TMP + 12),
                                                  ALU.mult, ALU.mult))
                for e in range(E3):
                    ins = v.tensor_scalar(col(RB + GT * e), col(TMP + 16), gwb[:, e:e + 1], gbb[:, e:e + 1], ALU.mult, ALU.add)
                route.link(ins)
                dve.wait_ge(s_lgc, r + 1)
                v.tensor_tensor(col(LL, 12), col(LL, 12), col(RB, 12), ALU.add)
                route.link(v.tensor_tensor(col(LL + 12, 12), p_acc[1][:, 32:44], col(RB, 12), ALU.add))
                a, b, c_ = (col(LL + GT * e) for e in range(E3))
                v.tensor_tensor(col(TMP + 20), a, b, ALU.max)
                route.link(v.tensor_tensor(col(TMP + 24), a, b, ALU.min))
                v.tensor_tensor(col(TMP + 28), col(TMP + 20), c_, ALU.max)
                route.link(v.tensor_tensor(col(TMP + 32), col(TMP + 20), c_, ALU.min))
                v.tensor_tensor(col(TMP + 36), col(TMP + 24), col(TMP + 32), ALU.max)
                route.link(v.tensor_tensor(col(TMP + 40), col(TMP + 24), c_, ALU.min))
                v.tensor_tensor(rt[:, DD:DD + 8].rearrange("p (q j) -> p q j", q=2),
                                rt[:, TMP + 36:TMP + 44].rearrange("p (q j) -> p q j", q=2),
                                col(TMP + 28).unsqueeze(1).to_broadcast([P, 2, GT]), ALU.subtract).then_inc(s_dd, 1)
                a0, b0, c0 = (col(LL + 12 + GT * e) for e in range(E3))
                ab, ac, bc = (col(G + GT * n) for n in range(3))
                nab, nac, nbc = (col(NG + GT * n) for n in range(3))
                v.tensor_tensor(ab, a0, b0, ALU.is_ge)
                v.tensor_tensor(ac, a0, c0, ALU.is_ge)
                route.link(v.tensor_tensor(bc, b0, c0, ALU.is_ge))
                route.link(v.tensor_scalar(col(NG, 12), col(G, 12), -1.0, 1.0, ALU.mult, ALU.add))
                for n, (x, y) in enumerate(((ab, ac), (nab, bc), (nac, nbc))):
                    v.tensor_tensor(col(I1 + GT * n), x, y, ALU.mult)
                for n, (x, y) in enumerate(((nab, nac), (ab, nbc), (ac, bc))):
                    ins = v.tensor_tensor(col(I3 + GT * n), x, y, ALU.mult)
                route.link(ins)
                route.link(v.tensor_tensor(col(NG, 12), col(I1, 12), col(I3, 12), ALU.add))
                route.link(v.tensor_scalar(col(I3, 12), col(NG, 12), -1.0, 1.0, ALU.mult, ALU.add))
                dve.wait_ge(s_ee, r + 1)
                route.link(v.tensor_scalar(col(TMP + 20), col(EE), 1.0, None, ALU.add))
                route.link(v.tensor_tensor(col(TMP + 24), col(TMP + 20), col(EE + 4), ALU.add))
                route.link(v.scalar_tensor_tensor(col(TMP + 28), col(TMP + 24), 1e-8, col(TMP + 20), ALU.mult, ALU.add))
                route.link(v.reciprocal(col(TMP + 32), col(TMP + 28)))
                route.link(v.tensor_tensor(col(TMP + 36), col(EE), col(TMP + 32), ALU.mult))
                v.tensor_tensor(three(G), three(I1), col(TMP + 32).unsqueeze(1).to_broadcast([P, E3, GT]), ALU.mult)
                route.link(v.tensor_tensor(three(NG), three(I3), col(TMP + 36).unsqueeze(1).to_broadcast([P, E3, GT]), ALU.mult))
                v.tensor_tensor(col(OUT, 12), col(G, 12), col(NG, 12), ALU.add).then_inc(s_g, 1)
                assert route.k == ROUTE_LINKS, route.k
                dve.wait_ge(s_gth, r + 1)
                v.tensor_tensor(gtl[:], p_acc[0][0:E3, :], gth[:].bitcast(F32), ALU.subtract).then_inc(s_gtl, 1)
                for f in range(F3):
                    e = f // FT
                    dve.wait_ge(s_act, r * F3 + f + 1)
                    dve.wait_ge(s_gbc, r * E3 + e + 1)
                    v.tensor_tensor(hf[:, f % 2], sil[:, f % 2], gbc[:, e], ALU.mult).then_inc(s_hf3, 1)
                    dve.wait_ge(s_hh3, r * F3 + f + 1)
                    v.tensor_tensor(hl[:, f % HSLOTS], hf[:, f % 2], hh[:, f % HSLOTS].bitcast(F32), ALU.subtract).then_inc(s_hl3, 1)
                if not last:
                    x_lo(r + GROUPS + 1)
                    t_rows(r + GROUPS + 1)
                residual(r + GROUPS, s_down3, (r + 1) * F3)

            ROUTE_LINKS = 21
            with dve.Fori(0, GROUPS - 1) as r:
                group3(r)
            group3(GROUPS - 1, True)

        @block.tensor
        def _(pe):
            mm = nc.tensor.matmul

            pe.wait_ge(d_cond, 48)
            mm(bank[2][0:BATCH, 256:256 + CH], condt[:], cwt[:], start=True, stop=True).then_inc(s_ctx, 1)
            pe.wait_ge(d_mlp, 64)
            for l in range(COND_LAYERS):
                mm(bank[0][:, l * BATCH:(l + 1) * BATCH], mw01[:, l, 0], condt[:], start=True, stop=True).then_inc(s_m1, 1)
            pe.wait_ge(s_g1, COND_LAYERS)
            for l in range(COND_LAYERS):
                mm(bank[1][:, l * BATCH:(l + 1) * BATCH], mw01[:, l, 1], hid1[:, l], start=True, stop=True).then_inc(s_m2, 1)
            pe.wait_ge(s_ctxs, 1)
            pe.wait_ge(s_g2, COND_LAYERS)
            for l in range(COND_LAYERS):
                last = mm(bank[2][0:BATCH, l * MIX:(l + 1) * MIX], hid2[:, l], mw2[:, l], start=True, stop=True)
            last.then_inc(s_m3, 1)
            pe.wait_ge(s_at, 1)
            pe.wait_ge(s_const, 11)
            for l in range(COND_LAYERS):
                last = nc.tensor.transpose(bank[3][0:MIX, l * BATCH:(l + 1) * BATCH], att[:, l], ident[0:BATCH, 0:BATCH])
            last.then_inc(s_att, 1)
            pe.wait_ge(d_mix, 32)
            pe.wait_ge(s_atc, 1)
            for l in range(COND_LAYERS):
                mm(bank[2][0:BATCH, l * CH:(l + 1) * CH], attt[:, l], mixb[:, l], start=True, stop=True)
            for l in range(COND_LAYERS):
                lo, hi = ((4, 5), (6, 7), (4, 5))[l]
                if l == 2:
                    pe.wait_ge(s_agc, 3)
                mm(bank[lo][0:BATCH, :], attt[:, l], mixw[:, l, 0:512], start=True, stop=True)
                mm(bank[hi][0:BATCH, :], attt[:, l], mixw[:, l, 512:AGW], start=True, stop=True).then_inc(s_ag, 1)

            def conv(t):
                pe.wait_ge(s_tapl, t + 1)
                if not (isinstance(t, int) and t == 0):
                    pe.wait_ge(s_t0f, t)
                for b in range(BPT):
                    dst = p_cv[:].rearrange("p (a b c) -> p a b c", a=PH, b=BPT)[:, :, b, :]
                    n = 0
                    for j in range(SHIFTS):
                        for x, w in ((taph, cvh), (taph, cvl), (tapl, cvh)):
                            last = mm(dst, x[:, b, j:j + P], w[:, j].rearrange("p (a c) -> p a c", a=PH),
                                      start=(n == 0), stop=(n == 3 * SHIFTS - 1))
                            n += 1
                last.then_inc(s_cv, 1)

            pe.wait_ge(s_cvs, 2)
            conv(0)
            pe.wait_ge(s_constv, 3)
            pe.wait_ge(s_agc, 6)
            pe.wait_ge(s_wqr, KT)
            for k in range(KT):
                for o in range(KT):
                    last = nc.tensor.transpose(bank[7 - k // 2][:].bitcast(BF16)[:, (k % 2) * D + o * P:(k % 2) * D + (o + 1) * P],
                                               wq_rows[:, o, k * P:(k + 1) * P], identb[:])
                last.then_inc(s_wqt, 1)
            pe.wait_ge(s_gas, 2)
            pe.wait_ge(s_w0s, 2)

            def features(dst, weights, width, stop):
                n = 0
                for k in range(PH):
                    for x, w in ((t0h, weights[0]), (t0h, weights[1]), (t0l, weights[0])):
                        last = mm(dst[:, 0:width], x[:, k], w[:, k, :], start=(n == 0), stop=(stop and n == 3 * PH - 1),
                                  skip_group_check=not stop)
                        n += 1
                return last

            def step(t, conv_=True, tile=True):
                later = not (isinstance(t, int) and t == 0)
                later2 = not (isinstance(t, int) and t <= 1)
                if tile:
                    pe.wait_ge(s_t0l, t + 1)
                    if later:
                        pe.wait_ge(s_hm, t)
                    features(p_ga, (gah, gal), ER + E0, True).then_inc(s_ga, 1)
                    if later:
                        pe.wait_ge(s_x1, t)
                    features(p_y0, (w0h, w0l), D, False).then_inc(s_base, 1)
                if later:
                    pe.wait_ge(s_x1l, t)
                    pe.wait_ge(s_bdl, t)
                    if later2:
                        pe.wait_ge(s_c1, t - 1)
                    slot = BD_SLOT[0]
                    for n, (w, x) in enumerate(parts((bdh[:, slot], bdl[:, slot]), (x1h[:], x1l[:]))):
                        last = mm(p_c1[:], w, x, start=(n == 0), stop=(n == 2))
                    last.then_inc(s_cd1, 1)
                if conv_:
                    conv(t + 1)
                if tile:
                    pe.wait_ge(s_hml, t + 1)
                    if later:
                        pe.wait_ge(s_htc, t)
                    for a, src in enumerate((hmh, hml)):
                        for b in range(2):
                            last = nc.tensor.transpose(p_ht[0:HB, (2 * a + b) * P:(2 * a + b + 1) * P].bitcast(F32R),
                                                       src[:, b * HB:(b + 1) * HB], identr[:])
                    last.then_inc(s_ht, 1)
                if later:
                    pe.wait_ge(s_qb, t)
                    if later2:
                        pe.wait_ge(s_qtc, t - 1)
                    for k in range(KT):
                        last = nc.tensor.transpose(p_qt[:].bitcast(BF16)[:, k * P:(k + 1) * P], qb[:, k * P:(k + 1) * P], identb[:])
                    last.then_inc(s_qt, 1)
                if tile:
                    pe.wait_ge(s_htc, t + 1)
                    pe.wait_ge(s_lbs, 2)
                    for b in range(2):
                        for n, (x, w) in enumerate(((hts[:, 0, b], lbh[:, b]), (hts[:, 0, b], lbl[:, b]), (hts[:, 1, b], lbh[:, b]))):
                            last = mm(p_y0[:], x, w, start=False, stop=(b == 1 and n == 2), skip_group_check=True)
                    last.then_inc(s_y0, 1)
                if later:
                    pe.wait_ge(s_qtc, t)
                    if later2:
                        pe.wait_ge(s_x2, t - 1)
                    pe.wait_ge(s_wqc, KT)
                    for k in range(KT):
                        last = mm(p_y1[:], qt[:, k], wq[:, k], start=(k == 0), stop=(k == KT - 1))
                    last.then_inc(s_y1, 1)

            BD_SLOT = [0]
            step(0)
            step(1)
            BD_SLOT[0] = 1
            step(2)
            with pe.Fori(1, 6) as i:
                BD_SLOT[0] = 0
                step(i * 2 + 1)
                BD_SLOT[0] = 1
                step(i * 2 + 2)
            BD_SLOT[0] = 0
            step(13)
            BD_SLOT[0] = 1
            step(14)
            BD_SLOT[0] = 0
            step(15, conv_=False)
            BD_SLOT[0] = 1
            step(16, conv_=False, tile=False)

            def cond(c):
                pe.wait_ge(s_gl, c + 1)
                for j in range(GT):
                    if j < 2:
                        pe.wait_ge(s_xclp, c * 2 + j + 1)
                    else:
                        pe.wait_ge(s_xcld, c * 2 + j - 1)
                    for kt in range(KT):
                        cols = slice(kt * P, (kt + 1) * P)
                        xp = (xch[:, j % 2, cols], xcl[:, j % 2, cols])
                        for n, (x, w) in enumerate(parts(xp, (bdh[:, j], bdl[:, j]))):
                            last = mm(p_pre[kt][:, j * P:(j + 1) * P], x, w, start=(n == 0), stop=(n == 2))
                    last.then_inc(s_cond, 1)

            def wait_t(c, kt):
                pe.wait_ge(s_tlp if kt % 2 else s_tld, c * 2 + kt // 2 + 1)

            pe.wait_ge(s_x2, TILES)
            cond(0)

            def down2(s, m):
                pe.wait_ge(s_hl, s * MT + m + 1)
                for j in range(GT):
                    for n, h in enumerate((hh, hl)):
                        last = mm(p_acc[j][:], h[:, m % HSLOTS, j * P:(j + 1) * P], wdr[:, m],
                                  start=(m == 0 and n == 0), stop=(m == MT - 1 and n == 1), skip_group_check=True)
                last.then_inc(s_down, 1)

            with pe.Fori(0, GROUPS) as s:
                pe.wait_ge(d_wg, 32)
                pe.wait_ge(d_wd, 16)
                for m in range(MT):
                    for w, reader, done, b in ((wgr, s_sil, s_gate, 0), (wur, s_hf, s_up, 1)):
                        if m >= 2:
                            pe.wait_ge(reader, s * MT + m - 1)
                        for kt in range(KT):
                            if m == 0 and b == 0:
                                wait_t(s, kt)
                            for n, x in enumerate((th, tl)):
                                last = mm(p_pre[2 * (m % 2) + b][:], w[:, kt, m * P:(m + 1) * P], x[:, kt],
                                          start=(kt == 0 and n == 0), stop=(kt == KT - 1 and n == 1))
                        last.then_inc(done, 1)
                    if m >= LAG2:
                        down2(s, m - LAG2)
                pe.wait_ge(s_hf, (s + 1) * MT)
                cond(s + 1)
                for m in range(MT - LAG2, MT):
                    down2(s, m)

            def pre3(r, f):
                e, ft = divmod(f, FT)
                if f == 0:
                    pe.wait_ge(s_w3, 16)
                if f == 2 * FT:
                    pe.wait_ge(s_w3, 32)
                if f >= 4:
                    pe.wait_ge(s_act, r * F3 + f - 3)
                wh, wl = (w1bh, w1bl) if e == 2 else (w1ah[:, e], w1al[:, e])
                for kt in range(KT):
                    cols = slice(ft * P, (ft + 1) * P)
                    for n, (w, x) in enumerate(parts((wh[:, kt, cols], wl[:, kt, cols]), (th[:, kt], tl[:, kt]))):
                        last = mm(p_pre[f % 4][:], w, x, start=(kt == 0 and n == 0), stop=(kt == KT - 1 and n == 2))
                last.then_inc(s_pre, 1)

            def down3(r, f):
                e, ft = divmod(f, FT)
                if ft == 0:
                    pe.wait_ge(s_w3, (24, 40, 48)[e])
                pe.wait_ge(s_hl3, r * F3 + f + 1)
                for j in range(GT):
                    cols = slice(j * P, (j + 1) * P)
                    hp = (hh[:, f % HSLOTS, cols], hl[:, f % HSLOTS, cols])
                    for n, (h, w) in enumerate(parts(hp, (w2h[:, e, ft], w2l[:, e, ft]))):
                        last = mm(p_acc[j][:], h, w, start=False, stop=(f == F3 - 1 and n == 2), skip_group_check=True)
                last.then_inc(s_down3, 1)

            def group3(r, last_=False):
                c = r + GROUPS
                pe.wait_ge(s_res, c * GT - 3)
                n = 0
                for kt in range(KT):
                    wait_t(c, kt)
                    for w, x in parts((gwh[:, kt], gwl[:, kt]), (th[:, kt], tl[:, kt])):
                        last = mm(p_acc[3][0:E3, :], w, x, start=(n == 0), stop=(n == 3 * KT - 1))
                        n += 1
                last.then_inc(s_lg, 1)
                pre3(r, 0)
                pe.wait_ge(s_ltf, r + 1)
                pe.wait_ge(s_res, c * GT - 2)
                for j in range(GT):
                    last = mm(p_acc[2][:, 4 * j:4 * j + E3], ltf[:, j * P:(j + 1) * P], ident[0:E3, 0:E3], start=True, stop=True)
                last.then_inc(s_lgt, 1)
                pre3(r, 1)
                pe.wait_ge(s_rs, 2 * r + 2)
                pe.wait_ge(s_lgc, r + 1)
                pe.wait_ge(s_res, c * GT - 1)
                for kt in range(KT):
                    mm(p_acc[1][:, 0:32].rearrange("p (q b) -> p q b", q=2), ones[:], rs[:, :, kt, :],
                       start=(kt == 0), stop=(kt == KT - 1))
                mm(p_acc[1][:, 32:44], first[:], rt[:, 0:12], start=True, stop=True).then_inc(s_stat, 1)
                pre3(r, 2)
                pe.wait_ge(s_g, r + 1)
                pe.wait_ge(s_res, c * GT)
                for j in range(GT):
                    last = nc.tensor.transpose(p_acc[0][0:E3, j * P:(j + 1) * P],
                                               rt[:, 120:132].rearrange("p (e j) -> p j e", e=E3)[:, j], ident[:])
                last.then_inc(s_gt, 1)
                pre3(r, 3)
                pe.wait_ge(s_gtl, r + 1)
                for e in range(E3):
                    for n, g in enumerate((gth, gtl)):
                        last = mm(p_acc[e + 1][:], selr[:, e], g[:], start=(n == 0), stop=(n == 1))
                    last.then_inc(s_gb, 1)
                pre3(r, 4)
                pe.wait_ge(s_gbc, (r + 1) * E3)
                for j in range(GT):
                    cols = slice(j * P, (j + 1) * P)
                    for n, (g, b) in enumerate(parts((gth[:, cols], gtl[:, cols]), (b2h[:], b2l[:]))):
                        mm(p_acc[j][:], g, b, start=(n == 0), stop=False, skip_group_check=True)
                down3(r, 0)
                for f in range(LAG3 + 1, F3):
                    pre3(r, f)
                    down3(r, f - LAG3)
                down3(r, F3 - LAG3)
                if not last_:
                    pe.wait_ge(s_act, (r + 1) * F3)
                    cond(c + 1)
                for f in range(F3 - LAG3 + 1, F3):
                    down3(r, f)

            with pe.Fori(0, GROUPS - 1) as r:
                group3(r)
            group3(GROUPS - 1, True)


_ORDER = ["x_rows", "x_taps", "cond_t", "fside", "cw_t", "conv_w", "l0_w", "l0_ga", "l0_lb",
          "mlp_w01", "mlp_w2", "mlp_b01", "mlp_b2", "mix_w", "mix_b", "l1_w", "l1_b",
          "wg", "wu", "wd", "gate_w", "gate_w_last", "gate_b", "w1", "b1", "w2", "b2"]


def kernel(**inputs):
    import numpy as _np
    import concourse.bacc as _bacc
    from concourse import mybir as _mybir
    from concourse.bass_utils import run_bass_kernel_spmd as _run

    v = {k: _np.asarray(a) for k, a in inputs.items()}

    def tiled(a):
        return a.reshape(a.shape[0] // P, P, *a.shape[1:]).swapaxes(0, 1)

    padded = _np.zeros((BATCH, CH, PH * MW), v["x"].dtype)
    padded[:, :, PH:PH + D] = v["x"]
    x_taps = padded.reshape(BATCH, CH, MW, PH).transpose(3, 1, 0, 2).reshape(P, BATCH, MW)
    w = v["L0_cond_weight"]
    gc = CH // CONV_GROUPS
    conv_w = _np.zeros((PH, CH, SHIFTS, PH, CH), w.dtype)
    for s in range(PH):
        for j in range(SHIFTS):
            for p in range(PH):
                if 0 <= PH * j + s - p < TAPS:
                    for g in range(CONV_GROUPS):
                        o = slice(g * gc, (g + 1) * gc)
                        conv_w[s, o, j, p, o] = w[o, :, PH * j + s - p].T
    lora_a = v["L0_ffn_lora_A"].reshape(ER, D)
    names = [f"L{l}_cond_" for l in (1, 2, 3)]
    host = {
        "x_rows": v["x"].reshape(TILES, P, D),
        "x_taps": x_taps,
        "cond_t": v["cond_128"].T,
        "fside": v["fside_S_0"],
        "cw_t": v["L0_cond_c_weight"].T,
        "conv_w": conv_w.reshape(P, SHIFTS, P),
        "l0_w": v["L0_ffn_base_W"].reshape(D, P, PH).transpose(1, 2, 0),
        "l0_ga": _np.concatenate([lora_a, v["L0_ffn_gate_W"]]).reshape(ER + E0, P, PH).transpose(1, 2, 0),
        "l0_lb": v["L0_ffn_lora_B"].transpose(0, 2, 1).reshape(2, HB, D).transpose(1, 0, 2),
        "mlp_w01": _np.stack([_np.stack([v[n + "W0"], v[n + "W1"]], 1) for n in names], 1),
        "mlp_w2": _np.stack([v[n + "W2"] for n in names], 1),
        "mlp_b01": _np.stack([_np.stack([v[n + "b0"], v[n + "b1"]], 1) for n in names], 1),
        "mlp_b2": _np.stack([v[n + "b2"] for n in names]),
        "mix_w": _np.stack([v[n + "weight"][..., 0].transpose(0, 2, 1).reshape(MIX, AGW) for n in names], 1),
        "mix_b": _np.stack([v[n + "bias_k"] for n in names], 1),
        "l1_w": tiled(v["L1_ffn_w"]),
        "l1_b": v["L1_ffn_b"],
        "wg": tiled(v["L2_ffn_W_gate"].T),
        "wu": tiled(v["L2_ffn_W_up"].T),
        "wd": tiled(v["L2_ffn_W_down"].T),
        "gate_w": tiled(v["L3_ffn_gate_w"][:D]),
        "gate_w_last": v["L3_ffn_gate_w"][D],
        "gate_b": v["L3_ffn_gate_b"],
        "w1": v["L3_ffn_w1"].reshape(E3, KT, P, D).transpose(2, 0, 1, 3),
        "b1": v["L3_ffn_b1"].reshape(F3, P).T,
        "w2": v["L3_ffn_w2"].reshape(E3, FT, P, D).transpose(2, 0, 1, 3),
        "b2": v["L3_ffn_b2"],
    }

    nc = _bacc.Bacc("TRN2", target_bir_lowering=False, num_devices=1)
    arrays, args = {}, []
    for name in _ORDER:
        a = _np.ascontiguousarray(host[name])
        arrays[f"in_{name}_dram"] = a
        args.append(nc.dram_tensor(f"in_{name}_dram", a.shape, _mybir.dt.from_np(a.dtype), kind="ExternalInput").ap())
    out = nc.dram_tensor("out_0_dram", (TILES, P, D), F32, kind="ExternalOutput").ap()
    build(nc, *args, out)
    r = _run(nc, [arrays], core_ids=[0])
    return r.results[0]["out_0_dram"].reshape(BATCH, CH, D)
```

```python
from contextlib import ExitStack

import concourse.bass as bass
from concourse import mybir

F32 = mybir.dt.float32
F32R = mybir.dt.float32r
BF16 = mybir.dt.bfloat16
U32 = mybir.dt.uint32
ALU = mybir.AluOpType
ACT = mybir.ActivationFunctionType
AX = mybir.AxisListType

P = 128
BATCH, CH, D = 64, 32, 512
BPT = P // CH
TILES = BATCH // BPT
GT = 4
GROUPS = TILES // GT
GTOK = GT * P
KT = D // P
TAPS, CONV_GROUPS = 9, 4
PH = 4
SHIFTS = 3
MW = P + SHIFTS - 1
E0, RANK = 28, 8
ER = E0 * RANK
HB = ER // 2
LORA_SCALE = 2.0
MIX = 8
HID = 128
COND_LAYERS = 3
AGW = CH * CH
AGB = AGW + CH
QMAX, QEPS = 127.0, 1e-8
MAGIC = 1.5 * 2.0 ** 23
M2 = 1792
MT = M2 // P
W2_CHUNKS = 7
E3 = 3
FT = D // P
F3 = E3 * FT
VIS = int(CH * 0.3)
ES = 64 + E3
LATE3 = 3
LAG2, LAG3 = 3, 5
HSLOTS = 4


class Chain:

    def __init__(self, eng, sem):
        self.eng, self.sem, self.base, self.k = eng, sem, 0, 0

    def begin(self, base):
        self.base, self.k = base, 0

    def link(self, ins):
        self.k += 1
        ins.then_inc(self.sem, 1)
        self.eng.wait_ge(self.sem, self.base + self.k)


def parts(a, b):
    (ah, al), (bh, bl) = a, b
    return ((ah, bh), (ah, bl), (al, bh))


def build(nc, x_rows, x_taps, cond_t, fside, cw_t, conv_w, l0_w, l0_ga, l0_lb,
          mlp_w01, mlp_w2, mlp_b01, mlp_b2, mix_w, mix_b, l1_w, l1_b,
          wg, wu, wd, gate_w, gate_w_last, gate_b, w1, b1, w2, b2, out):
    with ExitStack() as ctx:
        def sb(name, shape, dt, stack=ctx):
            return stack.enter_context(nc.sbuf_tensor(name, shape, dt))

        def sem(name):
            return ctx.enter_context(nc.semaphore(name))

        xd = nc.dram_tensor("xd", [2 * TILES, P, D], F32, kind="Internal").ap()
        aggd = nc.dram_tensor("aggd", [COND_LAYERS * BATCH, AGB], F32, kind="Internal").ap()
        ctxd = nc.dram_tensor("ctxd", [2, BATCH * CH], F32, kind="Internal").ap()
        swd = nc.dram_tensor("swd", [KT, P], F32, kind="Internal").ap()

        xc = sb("xc", [P, 2, D], F32)
        with ExitStack() as st:
            swb = sb("swb", [P, D], F32, st)
            b1b = sb("b1b", [P, D], F32, st)
            cvx = sb("cvx", [P, 2, P * PH // 2], F32, st)
            bias0 = sb("bias0", [2, 2, P], F32R, st)
            bias0f = sb("bias0f", [2, 2, P], F32, st)
        xres = sb("xres", [P, GT, D], F32)
        ag1 = sb("ag1", [P, TILES, CH], F32)
        ag23 = sb("ag23", [P, 2 * TILES, CH], F32)
        bcol1 = sb("bcol1", [P, TILES], F32)
        onesr = sb("onesr", [2, P], F32R)
        bias23 = sb("bias23", [P, GTOK], F32)
        bdf = sb("bdf", [P, GT, P], F32)
        bdh = sb("bdh", [P, GT, P], F32R)
        bdl = sb("bdl", [P, GT, P], F32R)
        mask4 = sb("mask4", [P, BPT], F32)
        ident = sb("ident", [P, P], F32)
        identr = sb("identr", [P, P], F32R)
        identb = sb("identb", [P, P], BF16)
        ones = sb("ones", [P, P], F32)
        first = sb("first", [P, P], F32)
        selr = sb("selr", [ES, E3, P], F32R)
        fold = sb("fold", [2 * E3, E3], F32)
        iota = sb("iota", [P, E0], F32)
        gwp = sb("gwp", [P, KT, 2 * E3], F32R)
        gwb = sb("gwb", [P, E3], F32)
        gbb = sb("gbb", [P, E3], F32)
        b1c = sb("b1c", [P, F3], F32)
        b2s = sb("b2s", [ES, D], F32R)
        sx = sb("sx", [P, 4], F32)

        with ExitStack() as st:
            conv_raw = sb("conv_raw", [P, SHIFTS, P], F32, st)
            sel = sb("sel", [ES, E3, P], F32, st)
            ga_raw = sb("ga_raw", [P, KT, ER + E0], F32, st)
            w0_raw = sb("w0_raw", [P, KT, D], F32, st)
            lb_raw = sb("lb_raw", [HB, 2, D], F32, st)
            w1_raw = sb("w1_raw", [P, KT, D], F32, st)
            wq_rows = sb("wq_rows", [P, KT, D], BF16, st)
            gw_raw = sb("gw_raw", [P, KT, E3], F32, st)
            b2_raw = sb("b2_raw", [ES, D], F32, st)
            condt = sb("condt", [P, BATCH], F32, st)
            cwt = sb("cwt", [P, CH], F32, st)
            fsb = sb("fsb", [BATCH, CH], F32, st)
            mw01 = sb("mw01", [P, COND_LAYERS, 2, HID], F32, st)
            mw2 = sb("mw2", [P, COND_LAYERS, MIX], F32, st)
            mb01 = sb("mb01", [P, COND_LAYERS, 2], F32, st)
            mb2 = sb("mb2", [BATCH, COND_LAYERS, MIX], F32, st)
            mixw = sb("mixw", [MIX, COND_LAYERS, AGW], F32, st)
            mixb = sb("mixb", [MIX, COND_LAYERS, CH], F32, st)
            hid1 = sb("hid1", [P, COND_LAYERS, BATCH], F32, st)
            hid2 = sb("hid2", [P, COND_LAYERS, BATCH], F32, st)
            att = sb("att", [BATCH, COND_LAYERS, MIX], F32, st)
            atte = sb("atte", [BATCH, COND_LAYERS, MIX], F32, st)
            attm = sb("attm", [BATCH, 3, COND_LAYERS], F32, st)
            attt = sb("attt", [MIX, COND_LAYERS, BATCH], F32, st)
            aggs = sb("aggs", [BATCH, 2, AGB], F32, st)
            ctxs = sb("ctxs", [BATCH, CH], F32, st)
            ctxp = sb("ctxp", [BATCH, 2, CH], F32R, st)
            wsc = sb("wsc", [P, 3, KT], F32, st)
        with ExitStack() as st:
            w2h = sb("w2h", [P, E3, FT, D], F32R, st)
            w2l = sb("w2l", [P, E3, FT, D], F32R, st)
        wgr = sb("wgr", [P, KT, M2], F32R)
        wur = sb("wur", [P, KT, M2], F32R)

        with ExitStack() as st:
            w1bh = sb("w1bh", [P, KT, D], F32R, st)
            w1bl = sb("w1bl", [P, KT, D], F32R, st)
            gbc = sb("gbc", [P, E3, GTOK], F32, st)
            ltf = sb("ltf", [2 * E3, GTOK], F32, st)
            gp = sb("gp", [P, GT, ES], F32, st)
            gts = sb("gts", [ES, GTOK], F32R, st)
            rs = sb("rs", [P, 2, KT, GT * BPT], F32, st)
            rt = sb("rt", [P, 240], F32, st)
        wdr = sb("wdr", [P, MT, D], F32R)
        sb("rest3", [P, 384], F32)
        with ExitStack() as st:
            cvw = sb("cvw", [P, SHIFTS, 2, P], F32R, st)
            cvh, cvl = cvw[:, :, 0], cvw[:, :, 1]
            tap = sb("tap", [P, 2, BPT, MW], F32, st)
            taph = sb("taph", [P, BPT, MW], F32R, st)
            tapl = sb("tapl", [P, BPT, MW], F32R, st)
            gah = sb("gah", [P, KT, ER + E0], F32R, st)
            gal = sb("gal", [P, KT, ER + E0], F32R, st)
            w0h = sb("w0h", [P, KT, D], F32R, st)
            w0l = sb("w0l", [P, KT, D], F32R, st)
            lbh = sb("lbh", [HB, 2, D], F32R, st)
            lbl = sb("lbl", [HB, 2, D], F32R, st)
            t0f = sb("t0f", [P, PH, P], F32, st)
            t0h = sb("t0h", [P, PH, P], F32R, st)
            t0l = sb("t0l", [P, PH, P], F32R, st)
            hm = sb("hm", [P, ER], F32, st)
            hmh = sb("hmh", [P, ER], F32R, st)
            hml = sb("hml", [P, ER], F32R, st)
            hts = sb("hts", [HB, 2, 2, P], F32R, st)
            bd1f = sb("bd1f", [P, 2, P], F32, st)
            bd1h = sb("bd1h", [P, 2, P], F32R, st)
            bd1l = sb("bd1l", [P, 2, P], F32R, st)
            wq = sb("wq", [P, KT, D], BF16, st)
            xin = sb("xin", [P, 2, D], F32, st)
            lg = sb("lg", [P, E0], F32, st)
            mx8 = sb("mx8", [P, 8], F32, st)
            ix8 = sb("ix8", [P, 8], U32, st)
            gs = sb("gs", [P, 8], F32, st)
            g0 = sb("g0", [P, 3, E0], F32, st)
            x1 = sb("x1", [P, D], F32, st)
            x1h = sb("x1h", [P, D], F32R, st)
            x1l = sb("x1l", [P, D], F32R, st)
            x1b = sb("x1b", [P, D], F32, st)
            c1 = sb("c1", [P, D], F32, st)
            qb = sb("qb", [P, D], BF16, st)
            qt = sb("qt", [P, KT, P], BF16, st)
            yt = sb("yt", [P, D], F32, st)
            xo = sb("xo", [P, 2, D], F32, st)
        xch = sb("xch", [P, 2, D], F32R)
        xcl = sb("xcl", [P, 2, D], F32R)
        tf = sb("tf", [P, KT, GTOK], F32)
        th = sb("th", [P, KT, GTOK], F32R)
        tl = sb("tl", [P, KT, GTOK], F32R)
        hh = sb("hh", [P, HSLOTS, GTOK], F32R)
        hl = sb("hl", [P, HSLOTS, GTOK], F32R)
        sil = sb("sil", [P, 2, GTOK], F32)
        hf = sil
        raw3 = sb("raw3", [P, KT // 2, D], F32)
        w1ah = sb("w1ah", [P, 2, KT, D], F32R)
        w1al = sb("w1al", [P, 2, KT, D], F32R)

        bank = [ctx.enter_context(nc.psum_tensor(f"bank{i}", [P, 512], F32)) for i in range(8)]
        p_cv = (bank[0], bank[7])
        p_ga, p_ht, p_y0, p_c1, p_qt, p_y1 = bank[1:7]
        p_acc, p_pre = bank[4:8], bank[0:4]

        d_cond, d_mlp, d_mix, d_conv, d_ga, d_w0, d_lb, d_w1, d_l3 = (
            sem(f"d_{n}") for n in "cond mlp mix conv ga w0 lb w1 l3".split())
        d_sw, d_swb, d_ctx, d_agg, d_tab, d_b1b = (sem(f"d_{n}") for n in "sw swb ctx agg tab b1b".split())
        s_const = sem("s_const")
        s_constv = sem("s_constv")
        s_cvs, s_gas, s_w0s, s_lbs, s_l3s = (sem(f"s_{n}") for n in "cvs gas w0s lbs l3s".split())
        s_ctx, s_ctxs, s_m1, s_g1, s_m2, s_g2, s_m3, s_lm, s_ex, s_at, s_att, s_atc, s_ag, s_agc = (
            sem(f"s_{n}") for n in "ctx ctxs m1 g1 m2 g2 m3 lm ex at att atc ag agc".split())
        s_sw, s_wqr, s_wqt, s_wqc = (sem(f"s_{n}") for n in "sw wqr wqt wqc".split())
        ch_set = sem("ch_set")
        d_tap, d_xin, d_b0, d_st1 = ([sem(f"d_{n}{i}") for i in range(2)] for n in "tap xin b0 st1_".split())
        (s_b0, s_taph, s_tapl, s_cv, s_cvx, s_yt, s_t0f, s_t0h, s_t0l, s_ga, s_gd, s_ge, s_hm, s_hmh, s_hml, s_base, s_ht, s_htc,
         s_y0, s_x1, s_x1h, s_x1l, s_x1b, s_bdf, s_bdh, s_bdl, s_cd1, s_c1, s_qb, s_qt, s_qtc, s_y1, s_x2) = (
            sem(f"s1_{n}") for n in ("b0 taph tapl cv cvx yt t0f t0h t0l ga gd ge hm hmh hml base ht htc "
                                     "y0 x1 x1h x1l x1b bdf bdh bdl cd1 c1 qb qt qtc y1 x2").split())
        ch_gate, ch_q = sem("ch_gate"), sem("ch_q")
        d_xc = [sem(f"d_xc{i}") for i in range(2)]
        d_bias, d_xres, d_st = sem("d_bias"), sem("d_xres"), sem("d_st")
        s_xch, s_xclp, s_xcld, s_gf, s_gh, s_gl, s_cond, s_tf, s_th, s_tld, s_tlp, s_res = (
            sem(f"s2_{n}") for n in "xch xclp xcld gf gh gl cond tf th tld tlp res".split())
        d_w2, d_raw = sem("d_w2"), sem("d_raw")
        d_late = [sem(f"d_late{i}") for i in range(2)]
        s_w3 = sem("s_w3")
        s_gate, s_up, s_sil, s_hf, s_hh, s_hl, s_down = (sem(f"s2_{n}") for n in "gate up sil hf hh hl down".split())
        (s_lg, s_ltf, s_lgt, s_lgc, s_rs, s_stat, s_dd, s_ee, s_g, s_gt, s_gth, s_gtl, s_gb, s_gbc, s_gp, s_sum) = (
            sem(f"s3_{n}") for n in "lg ltf lgt lgc rs stat dd ee g gt gth gtl gb gbc gp sum".split())
        s_pre, s_act, s_hf3, s_hh3, s_hl3, s_down3 = (sem(f"s3_{n}") for n in "pre act hf hh hl down".split())
        s_last = sem("s3_last")
        ch_rt = sem("ch_rt")

        block = ctx.enter_context(nc.Block())

        @block.sync
        def _(sp):
            sp.dma_start(condt[:], cond_t).then_inc(d_cond, 16)
            sp.dma_start(cwt[:], cw_t).then_inc(d_cond, 16)
            sp.dma_start(fsb[:], fside.partition_broadcast(BATCH)).then_inc(d_cond, 16)
            sp.dma_start(tap[:, 0], x_taps[:, 0:BPT, :]).then_inc(d_tap[0], 16)
            sp.dma_start(conv_raw[:], conv_w).then_inc(d_conv, 16)
            sp.dma_start(ga_raw[:], l0_ga).then_inc(d_ga, 16)
            sp.wait_ge(s_ctxs, 3)
            sp.dma_start(ctxd.rearrange("a (b c) -> b a c", c=CH), ctxp[:].bitcast(F32)).then_inc(d_ctx, 16)
            sp.dma_start(w0_raw[:], l0_w).then_inc(d_w0, 16)
            sp.wait_ge(d_ctx, 16)
            sp.dma_start(bias0f[:, 0], ctxd[:, 0:P]).then_inc(d_b0[0], 16)
            sp.dma_start(lb_raw[:], l0_lb).then_inc(d_lb, 16)
            sp.dma_start(mixw[:], mix_w).then_inc(d_mix, 16)
            sp.dma_start(mixb[:], mix_b).then_inc(d_mix, 16)
            sp.dma_start(xin[:, 0], x_rows[0]).then_inc(d_xin[0], 16)
            sp.dma_start(w1_raw[:], l1_w).then_inc(d_w1, 16)
            sp.dma_start(tap[:, 1], x_taps[:, BPT:2 * BPT, :]).then_inc(d_tap[1], 16)
            sp.dma_start(b1b[:], l1_b.partition_broadcast(P)).then_inc(d_b1b, 16)
            sp.dma_start(gw_raw[:], gate_w).then_inc(d_l3, 16)
            sp.wait_ge(s_const, 14)
            for n in range(3):
                sp.dma_start(b2_raw[32 * n:32 * n + E3, :], b2).then_inc(d_l3, 16)
            sp.dma_start(gwb[:], gate_w_last.partition_broadcast(P)).then_inc(d_l3, 16)
            sp.dma_start(gbb[:], gate_b.partition_broadcast(P)).then_inc(d_l3, 16)
            sp.dma_start(b1c[:], b1).then_inc(d_l3, 16)

            def tables(l):
                sp.wait_ge(s_agc, 3 * (l + 1))
                sp.dma_start(aggd[l * BATCH:(l + 1) * BATCH, :], aggs[:, l % 2]).then_inc(d_agg, 16)
                sp.wait_ge(d_agg, 16 * (l + 1))
                mixed = aggd[l * BATCH:(l + 1) * BATCH, :].rearrange("(t b) n -> b t n", b=BPT)
                for b in range(BPT):
                    rows = slice(CH * b, CH * (b + 1))
                    dst = ag1[rows] if l == 0 else ag23[rows, (l - 1) * TILES:l * TILES]
                    sp.dma_start(dst, mixed[b, :, 0:AGW].rearrange("t (i o) -> i t o", i=CH)).then_inc(d_tab, 16)
                    if l == 0:
                        sp.dma_start(bcol1[rows], mixed[b, :, AGW:AGB].rearrange("t o -> o t"),
                                     allow_slow_non_contiguous=True).then_inc(d_tab, 16)

            def step(t, p, load=True, tail=True):
                if load:
                    n = sp.snap((t + 2) * BPT)
                    sp.wait_ge(s_tapl, t + 1)
                    sp.dma_start(tap[:, p], x_taps[:, bass.ds(n, BPT), :]).then_inc(d_tap[p], 16)
                if tail:
                    if not (isinstance(t, int) and t == 0):
                        sp.wait_ge(s_b0, t)
                        sp.wait_ge(s_x1, t)
                    sp.dma_start(bias0f[:, 1 - p], ctxd[:, bass.ds((t + 1) * P, P)]).then_inc(d_b0[1 - p], 16)
                    sp.dma_start(xin[:, 1 - p], x_rows[bass.ds(t + 1, 1)].rearrange("a p d -> (a p) d")).then_inc(d_xin[1 - p], 16)
                if not (isinstance(t, int) and t <= 1):
                    sp.wait_ge(s_x2, t - 1)
                    sp.dma_start(xd[bass.ds(t - 2, 1)].rearrange("a p d -> (a p) d"), xo[:, p]).then_inc(d_st1[p], 16)

            step(0, 0)
            sp.wait_ge(s_sw, 1)
            sp.dma_start(swd.rearrange("k p -> p k"), wsc[:, 1, :], allow_slow_non_contiguous=True).then_inc(d_sw, 16)
            sp.wait_ge(d_sw, 16)
            sp.dma_start(swb[:], swd.rearrange("k p -> (k p)").partition_broadcast(P)).then_inc(d_swb, 16)
            tables(0)
            step(1, 1)
            tables(1)
            tables(2)
            step(2, 0)
            with sp.Fori(1, 6) as i:
                step(i * 2 + 1, 1)
                step(i * 2 + 2, 0)
            step(13, 1)
            step(14, 0, load=False)

            def load_xc(row, j):
                sp.dma_start(xc[:, j % 2], xd[bass.ds(row + j, 1)].rearrange("a p d -> (a p) d")).then_inc(d_xc[j % 2], 16)

            def load_bias(c):
                sp.dma_start(bias23[:].rearrange("p (b o) -> p b o", o=CH),
                             aggd[bass.ds(c * (GT * BPT) + BATCH, GT * BPT), AGW:AGB].partition_broadcast(P)).then_inc(d_bias, 16)

            for p in range(2):
                sp.wait_ge(d_st1[p], 16 * GT // 2)
            load_xc(0, 0)
            load_xc(0, 1)
            load_bias(0)
            step(15, 1, load=False, tail=False)
            sp.wait_ge(s_xch, 2)
            sp.wait_ge(s_xclp, 2)
            load_xc(0, 2)
            load_xc(0, 3)
            step(16, 0, load=False, tail=False)
            step(17, 1, load=False, tail=False)
            for p in range(2):
                sp.wait_ge(d_st1[p], 16 * TILES // 2)

            def load_next(c):
                row = sp.snap(c * GT)
                sp.wait_ge(s_tf, c * KT)
                load_bias(c)
                sp.wait_ge(s_xcld, c * 2)
                load_xc(row, 0)
                load_xc(row, 1)
                sp.wait_ge(s_xclp, c * 2 + 2)
                load_xc(row, 2)
                load_xc(row, 3)

            def load_xres(c):
                sp.dma_start(xres[:], xd[bass.ds(c * GT, GT)].rearrange("a p d -> p a d")).then_inc(d_xres, 16)

            sp.wait_ge(s_x2, TILES)
            load_xres(0)

            def group(c, r, dst):
                load_next(c + 1)
                sp.wait_ge(s_res, (c + 1) * GT)
                sp.dma_start(dst[bass.ds(r * GT, GT)].rearrange("a p d -> p a d"), xres[:]).then_inc(d_st, 16)
                sp.wait_ge(d_st, (c + 1) * 16)
                load_xres(c + 1)

            with sp.Fori(0, GROUPS) as s:
                group(s, s + GROUPS, xd)
            for n in range(LATE3 * KT):
                src = (w1[:, 2], w2[:, 1], w2[:, 2])[n // KT]
                sp.wait_ge(s_w3, 24 + max(2 * n - 2, 0))
                sp.dma_start(raw3[:, n % 2], src[:, n % KT]).then_inc(d_late[n % 2], 16)
            with sp.Fori(0, GROUPS - 1) as r:
                group(r + GROUPS, r, out)
            for j in range(GT):
                sp.wait_ge(s_res, (2 * GROUPS - 1) * GT + j + 1)
                sp.dma_start(out[(GROUPS - 1) * GT + j], xres[:, j]).then_inc(d_st, 16)
            sp.wait_ge(d_st, 16 * (2 * GROUPS - 1 + GT))

        @block.gpsimd
        def _(pool):
            nc.gpsimd.memset(ident[:], 0.0).then_inc(s_const, 1)
            nc.gpsimd.memset(mask4[:], 1.0).then_inc(s_const, 1)
            nc.gpsimd.memset(first[:], 0.0).then_inc(s_const, 1)
            nc.gpsimd.memset(sel[:], 0.0)
            nc.gpsimd.memset(fold[:], 0.0)
            nc.gpsimd.memset(b2_raw[:], 0.0).then_inc(s_const, 1)
            nc.gpsimd.memset(ones[:], 1.0).then_inc(s_const, 1)
            nc.gpsimd.iota(iota[:], [[1, E0]], base=0, channel_multiplier=0,
                           allow_small_or_imprecise_dtypes=True).then_inc(s_const, 1)
            pool.wait_ge(s_const, 6)
            nc.gpsimd.affine_select(out=ident[:], in_=ident[:], compare_op=ALU.not_equal, fill=1.0, base=0,
                                    pattern=[[-1, P]], channel_multiplier=1).then_inc(s_const, 1)
            nc.gpsimd.affine_select(out=mask4[:], in_=mask4[:], compare_op=ALU.is_ge, fill=0.0, base=0,
                                    pattern=[[-CH, BPT]], channel_multiplier=1).then_inc(s_const, 1)
            nc.gpsimd.affine_select(out=first[:].rearrange("p (b c) -> p b c", c=CH),
                                    in_=first[:].rearrange("p (b c) -> p b c", c=CH), compare_op=ALU.not_equal,
                                    fill=1.0, base=0, pattern=[[-CH, BPT], [0, CH]], channel_multiplier=1).then_inc(s_const, 1)
            pool.wait_ge(s_const, 9)
            nc.gpsimd.affine_select(out=mask4[:], in_=mask4[:], compare_op=ALU.is_ge, fill=0.0, base=CH - 1,
                                    pattern=[[CH, BPT]], channel_multiplier=-1).then_inc(s_const, 1)
            pool.wait_ge(s_const, 10)
            for n in range(2):
                nc.gpsimd.affine_select(out=sel[:], in_=sel[:], compare_op=ALU.not_equal, fill=1.0, base=-32 * n,
                                        pattern=[[-1, E3], [0, P]], channel_multiplier=1).then_inc(s_const, 1)
                nc.gpsimd.affine_select(out=fold[:], in_=fold[:], compare_op=ALU.not_equal, fill=1.0, base=-E3 * n,
                                        pattern=[[-1, E3]], channel_multiplier=1).then_inc(s_const, 1)
                pool.wait_ge(s_const, 12 + 2 * n)

            def block_diag(dst, table):
                for n in range(dst.shape[1]):
                    ins = nc.gpsimd.tensor_tensor(
                        dst[:, n].rearrange("p (b o) -> p b o", b=BPT),
                        table[:, n:n + 1, :].to_broadcast([P, BPT, CH]),
                        mask4[:].unsqueeze(2).to_broadcast([P, BPT, CH]), ALU.mult)
                return ins

            def tap_lo(t, p):
                pool.wait_ge(s_taph, t + 1)
                nc.gpsimd.tensor_tensor(tapl[:], tap[:, p], taph[:].bitcast(F32), ALU.subtract).then_inc(s_tapl, 1)

            def diag_lo(t, p):
                pool.wait_ge(s_bdh, t + 1)
                nc.gpsimd.tensor_tensor(bd1l[:, p], bd1f[:, p], bd1h[:, p].bitcast(F32), ALU.subtract).then_inc(s_bdl, 1)

            def diag_tile(t, p):
                if isinstance(t, int) and t == 0:
                    pool.wait_ge(d_tab, 16 * 2 * BPT)
                if not (isinstance(t, int) and t < 2):
                    pool.wait_ge(s_cd1, t - 1)
                block_diag(bd1f[:, p:p + 1], ag1[:, bass.ds(t, 1)]).then_inc(s_bdf, 1)

            def diag_group(c, first_=False):
                if not first_:
                    pool.wait_ge(s_cond, c * GT)
                block_diag(bdf[:], ag23[:, bass.ds(c * GT, GT)]).then_inc(s_gf, 1)
                pool.wait_ge(s_gh, c + 1)
                nc.gpsimd.tensor_tensor(bdl[:], bdf[:], bdh[:].bitcast(F32), ALU.subtract).then_inc(s_gl, 1)

            def x_lo(c, j):
                pool.wait_ge(s_xch, c * GT + j + 1)
                nc.gpsimd.tensor_tensor(xcl[:, j % 2], xc[:, j % 2], xch[:, j % 2].bitcast(F32), ALU.subtract).then_inc(s_xclp, 1)

            def t_lo(c):
                for kt in (0, 2):
                    pool.wait_ge(s_th, c * KT + kt + 1)
                    nc.gpsimd.tensor_tensor(tl[:, kt], tf[:, kt], th[:, kt].bitcast(F32), ALU.subtract).then_inc(s_tlp, 1)

            W2_COLS = KT * M2 // W2_CHUNKS

            def load_w2(q, matrices):
                cols = bass.ds(q * W2_COLS, W2_COLS)
                for dst, src in matrices:
                    pool.dma_start(dst[:].rearrange("p k n -> p (k n)")[:, cols],
                                   src.rearrange("p k n -> p (k n)")[:, cols]).then_inc(d_w2, 16)

            def x_after_1(t, p, stored):
                pool.wait_ge(s_yt, t + 1)
                if not (isinstance(stored, int) and stored == 0):
                    pool.wait_ge(d_st1[p], stored * 16)
                pool.wait_ge(s_x1b, t + 1)
                nc.gpsimd.tensor_tensor(xo[:, p], yt[:], x1b[:], ALU.add).then_inc(s_x2, 1)

            def conv_bias(t, p, n):
                pool.wait_ge(d_b0[p], n * 16)
                if not (isinstance(t, int) and t <= 1):
                    pool.wait_ge(s_cv, 2 * t - 2)
                nc.gpsimd.tensor_tensor(bias0[:, p], bias0f[:, p], ones[0:2, :], ALU.mult).then_inc(s_b0, 1)

            def step(t, p, stored, ahead_=None, taps=True, tile=True, load=None):
                later = not (isinstance(t, int) and t == 0)
                if later:
                    pool.wait_ge(s_x1h, t)
                    nc.gpsimd.tensor_tensor(x1l[:], x1[:], x1h[:].bitcast(F32), ALU.subtract).then_inc(s_x1l, 1)
                    diag_lo(t - 1, 1 - p)
                if ahead_ is not None:
                    conv_bias(t + 1, 1 - p, ahead_)
                if later:
                    if not (isinstance(t, int) and t == 1):
                        x_after_1(t - 2, p, stored)
                        pool.wait_ge(s_x2, t - 1)
                    nc.gpsimd.tensor_tensor(x1b[:], x1[:], b1b[:], ALU.add).then_inc(s_x1b, 1)
                if load is not None:
                    load_w2(*load)
                if taps:
                    tap_lo(t + 2, p)
                if tile:
                    diag_tile(t, p)

            tap_lo(0, 0)
            pool.wait_ge(s_gas, 1)
            nc.gpsimd.tensor_tensor(gal[:], ga_raw[:], gah[:].bitcast(F32), ALU.subtract).then_inc(s_gas, 1)
            conv_bias(0, 0, 1)
            tap_lo(1, 1)
            pool.wait_ge(s_lbs, 1)
            nc.gpsimd.tensor_tensor(lbl[:], lb_raw[:], lbh[:].bitcast(F32), ALU.subtract).then_inc(s_lbs, 1)
            step(0, 0, 0, 1)
            pool.wait_ge(d_b1b, 16)
            step(1, 1, 0, 2)
            pool.wait_ge(d_agg, 16 * COND_LAYERS)
            pool.wait_ge(s_wqt, 4)
            pool.wait_ge(s_l3s, 4)
            pool.wait_ge(s_w0s, 2)
            down, gate_up = ((wdr, wd),), ((wgr, wg), (wur, wu))
            step(2, 0, 0, 2, load=(0, down + gate_up))
            step(3, 1, 0, 3, load=(1, down))
            step(4, 0, 1, 3, load=(1, gate_up))
            with pool.Fori(2, 6) as i:
                step(i * 2 + 1, 1, i - 1, i + 2, load=(i, down))
                step(i * 2 + 2, 0, i, i + 2, load=(i, gate_up))
            step(13, 1, 5, 8, load=(6, down))
            step(14, 0, 6, 8, taps=False, load=(6, gate_up))
            pool.wait_ge(d_tab, 16 * 4 * BPT)
            diag_group(0, True)
            step(15, 1, 6, taps=False)
            x_lo(0, 0)
            x_lo(0, 1)
            step(16, 0, 7, taps=False, tile=False)
            t_lo(0)
            x_after_1(15, 1, 7)

            def split3(n, hi, lo, src):
                for half in range(2):
                    done = 8 * n + 4 * half
                    if done:
                        pool.wait_ge(s_w3, done)
                    pool.dma_start(raw3[:], src[:, 2 * half:2 * half + 2]).then_inc(d_raw, 16)
                    pool.wait_ge(d_raw, 16 * (2 * n + half + 1))
                    for k in range(2):
                        nc.gpsimd.tensor_scalar(hi[:, 2 * half + k], raw3[:, k], 1.0, 1.0, ALU.mult, ALU.mult).then_inc(s_w3, 1)
                    for k in range(2):
                        pool.wait_ge(s_w3, done + k + 1)
                        nc.gpsimd.tensor_tensor(lo[:, 2 * half + k], raw3[:, k], hi[:, 2 * half + k].bitcast(F32),
                                                ALU.subtract).then_inc(s_w3, 1)

            pool.wait_ge(s_x2, TILES)
            for p in range(2):
                pool.wait_ge(d_st1[p], 16 * TILES // 2)

            def ahead(c):
                diag_group(c)
                x_lo(c, 0)
                x_lo(c, 1)
                t_lo(c)

            split3(0, w1ah[:, 0], w1al[:, 0], w1[:, 0])
            ahead(1)
            split3(1, w1ah[:, 1], w1al[:, 1], w1[:, 1])
            with pool.Fori(1, GROUPS) as s:
                ahead(s + 1)
            pool.wait_ge(s_up, MT * GROUPS)
            split3(2, w2h[:, 0], w2l[:, 0], w2[:, 0])
            pool.wait_ge(s_down, MT * GROUPS)
            for n in range(LATE3 * KT):
                hi, lo = ((w1bh, w1bl), (w2h[:, 1], w2l[:, 1]), (w2h[:, 2], w2l[:, 2]))[n // KT]
                pool.wait_ge(d_late[n % 2], 16 * (n // 2 + 1))
                nc.gpsimd.tensor_scalar(hi[:, n % KT], raw3[:, n % 2], 1.0, 1.0, ALU.mult, ALU.mult).then_inc(s_w3, 1)
                pool.wait_ge(s_w3, 24 + 2 * n + 1)
                nc.gpsimd.tensor_tensor(lo[:, n % KT], raw3[:, n % 2], hi[:, n % KT].bitcast(F32),
                                        ALU.subtract).then_inc(s_w3, 1)
            with pool.Fori(0, GROUPS - 1) as r:
                ahead(r + GROUPS + 1)

        @block.scalar
        def _(act):
            act.dma_start(mw01[:], mlp_w01).then_inc(d_mlp, 16)
            act.dma_start(mw2[:], mlp_w2).then_inc(d_mlp, 16)
            act.dma_start(mb01[:], mlp_b01).then_inc(d_mlp, 16)
            act.dma_start(mb2[:], mlp_b2.partition_broadcast(BATCH)).then_inc(d_mlp, 16)

            def tap_hi(t, p, n):
                act.wait_ge(d_tap[p], n * 16)
                if not (isinstance(t, int) and t == 0):
                    act.wait_ge(s_cv, 2 * t)
                nc.scalar.activation(taph[:], tap[:, p], ACT.Copy).then_inc(s_taph, 1)

            act.wait_ge(s_ctxs, 1)
            nc.scalar.activation(ctxp[:, 0], ctxs[:], ACT.Copy).then_inc(s_ctxs, 1)
            tap_hi(0, 0, 1)
            act.wait_ge(d_conv, 16)
            nc.scalar.activation(cvh, conv_raw[:], ACT.Copy).then_inc(s_cvs, 1)
            act.wait_ge(s_const, 14)
            nc.scalar.activation(onesr[:], ones[0:2, :], ACT.Copy).then_inc(s_constv, 1)
            act.wait_ge(d_mlp, 64)
            act.wait_ge(s_m1, COND_LAYERS)
            for l in range(COND_LAYERS):
                nc.scalar.activation(hid1[:, l], bank[2][:, l * BATCH:(l + 1) * BATCH], ACT.Gelu,
                                     bias=mb01[:, l, 0:1]).then_inc(s_g1, 1)
            act.wait_ge(d_ga, 16)
            nc.scalar.activation(gah[:], ga_raw[:], ACT.Copy).then_inc(s_gas, 1)
            act.wait_ge(s_m2, COND_LAYERS)
            for l in range(COND_LAYERS):
                nc.scalar.activation(hid2[:, l], bank[3][:, l * BATCH:(l + 1) * BATCH], ACT.Gelu,
                                     bias=mb01[:, l, 1:2]).then_inc(s_g2, 1)
            act.wait_ge(d_w0, 16)
            nc.scalar.activation(w0h[:], w0_raw[:], ACT.Copy).then_inc(s_w0s, 1)

            def mixed(l):
                act.wait_ge(s_ag, l + 1)
                if l == 2:
                    act.wait_ge(d_agg, 16)
                nc.scalar.activation(aggs[:, l % 2, 0:512], bank[4][0:BATCH, :], ACT.Copy).then_inc(s_agc, 1)
                nc.scalar.activation(aggs[:, l % 2, 512:AGW], bank[5][0:BATCH, :], ACT.Copy).then_inc(s_agc, 1)
                nc.scalar.activation(aggs[:, l % 2, AGW:AGB], bank[6][0:BATCH, l * CH:(l + 1) * CH], ACT.Copy).then_inc(s_agc, 1)

            def conv_extra(t):
                for h in range(2):
                    act.wait_ge(s_cv, 2 * t + h + 1)
                    if not (isinstance(t, int) and t == 0):
                        act.wait_ge(s_t0f, 2 * t)
                    nc.scalar.activation(cvx[:, h], p_cv[h][:, 256:512], ACT.Copy).then_inc(s_cvx, 1)

            def t0_hi(t):
                act.wait_ge(s_t0f, 2 * t + 2)
                if not (isinstance(t, int) and t == 0):
                    act.wait_ge(s_base, t)
                nc.scalar.activation(t0h[:], t0f[:], ACT.Copy).then_inc(s_t0h, 1)

            conv_extra(0)
            t0_hi(0)
            act.wait_ge(s_lm, 1)
            nc.scalar.activation(atte[:], att[:], ACT.Exp).then_inc(s_ex, 1)
            nc.scalar.activation(identr[:], ident[:], ACT.Copy).then_inc(s_constv, 1)
            nc.scalar.activation(identb[:], ident[:], ACT.Copy).then_inc(s_constv, 1)
            act.wait_ge(d_lb, 16)
            nc.scalar.activation(lbh[:], lb_raw[:], ACT.Copy).then_inc(s_lbs, 1)
            tap_hi(1, 1, 1)

            def diag_hi1(t, p):
                act.wait_ge(s_bdf, t + 1)
                nc.scalar.activation(bd1h[:, p], bd1f[:, p], ACT.Copy).then_inc(s_bdh, 1)

            def mixed1(t, later2=True):
                act.wait_ge(s_cd1, t)
                if later2:
                    act.wait_ge(s_qb, t - 1)
                act.wait_ge(d_tab, 16 * 2 * BPT)
                nc.scalar.activation(c1[:], p_c1[:], ACT.Identity, bias=bcol1[:, bass.ds(t - 1, 1)]).then_inc(s_c1, 1)

            def integers_t(t, later2=True):
                act.wait_ge(s_qt, t)
                if later2:
                    act.wait_ge(s_y1, t - 1)
                nc.scalar.activation(qt[:].rearrange("p a n -> p (a n)"), p_qt[:].bitcast(BF16)[:, 0:D], ACT.Copy).then_inc(s_qtc, 1)

            def step(t, p, k, tap_=True, conv=True):
                later = not (isinstance(t, int) and t == 0)
                later2 = not (isinstance(t, int) and t <= 1)
                if later:
                    act.wait_ge(s_x1, t)
                    if later2:
                        act.wait_ge(s_cd1, t - 1)
                    nc.scalar.activation(x1h[:], x1[:], ACT.Copy).then_inc(s_x1h, 1)
                    diag_hi1(t - 1, 1 - p)
                act.wait_ge(s_gd, t + 1)
                nc.scalar.activation(gs[:, 4:5], gs[:, 3:4], ACT.Exp).then_inc(s_ge, 1)
                if not later:
                    act.wait_ge(s_att, 1)
                    nc.scalar.activation(attt[:].rearrange("k l b -> k (l b)"), bank[5][0:MIX, 0:COND_LAYERS * BATCH],
                                         ACT.Copy).then_inc(s_atc, 1)
                act.wait_ge(s_hm, t + 1)
                if later:
                    act.wait_ge(s_ht, t)
                nc.scalar.activation(hmh[:], hm[:], ACT.Copy).then_inc(s_hmh, 1)
                if later:
                    mixed1(t, later2)
                else:
                    mixed(0)
                    mixed(1)
                act.wait_ge(s_ht, t + 1)
                if later:
                    act.wait_ge(s_y0, t)
                nc.scalar.activation(hts[:].rearrange("p a b n -> p (a b n)"), p_ht[0:HB, :], ACT.Copy).then_inc(s_htc, 1)
                if conv:
                    conv_extra(t + 1)
                if later:
                    integers_t(t, later2)
                if conv:
                    t0_hi(t + 1)
                if tap_:
                    tap_hi(t + 2, p, k + 1)
                if not later:
                    mixed(2)
                    nc.scalar.activation(selr[:], sel[:], ACT.Copy).then_inc(s_constv, 1)
                    act.wait_ge(d_l3, 16 * 7)
                    nc.scalar.activation(gwp[:, :, 0:E3], gw_raw[:], ACT.Copy).then_inc(s_l3s, 1)
                    nc.scalar.activation(b2s[:], b2_raw[:], ACT.Copy).then_inc(s_l3s, 1)

            step(0, 0, 1)
            step(1, 1, 1)
            step(2, 0, 2)
            with act.Fori(1, 6) as i:
                step(i * 2 + 1, 1, i + 1)
                step(i * 2 + 2, 0, i + 2)
            step(13, 1, 7)
            step(14, 0, 8, tap_=False)

            def x_hi(c, j, k, wait_cond=True):
                act.wait_ge(d_xc[j % 2], k)
                if wait_cond:
                    act.wait_ge(s_cond, c * GT + j - 1)
                nc.scalar.activation(xch[:, j % 2], xc[:, j % 2], ACT.Copy).then_inc(s_xch, 1)

            def diag_hi(c):
                act.wait_ge(s_gf, c + 1)
                nc.scalar.activation(bdh[:], bdf[:], ACT.Copy).then_inc(s_gh, 1)

            def t_hi(c):
                for kt in range(KT):
                    act.wait_ge(s_tf, c * KT + kt + 1)
                    nc.scalar.activation(th[:, kt], tf[:, kt], ACT.Copy).then_inc(s_th, 1)

            diag_hi(0)
            act.wait_ge(s_cv, 2 * TILES)
            x_hi(0, 0, 16, False)
            x_hi(0, 1, 16, False)
            step(15, 1, 8, tap_=False, conv=False)
            act.wait_ge(s_x1, TILES)
            act.wait_ge(s_cd1, TILES - 1)
            nc.scalar.activation(x1h[:], x1[:], ACT.Copy).then_inc(s_x1h, 1)
            diag_hi1(TILES - 1, 1)
            x_hi(0, 2, 32)
            x_hi(0, 3, 32)
            mixed1(TILES)
            integers_t(TILES)
            t_hi(0)

            def ahead(c):
                diag_hi(c)
                x_hi(c, 0, c * 32 + 16)
                x_hi(c, 1, c * 32 + 16)

            def boundary(c):
                x_hi(c, 2, c * 32 + 32)
                x_hi(c, 3, c * 32 + 32)
                t_hi(c)

            with act.Fori(0, GROUPS) as s:
                for m in range(MT):
                    act.wait_ge(s_gate, s * MT + m + 1)
                    if m >= 2:
                        act.wait_ge(s_hl, s * MT + m - 1)
                    nc.scalar.activation(sil[:, m % 2], p_pre[2 * (m % 2)][:], ACT.Silu).then_inc(s_sil, 1)
                    act.wait_ge(s_hf, s * MT + m + 1)
                    if m >= HSLOTS:
                        act.wait_ge(s_down, s * MT + m - HSLOTS + 1)
                    nc.scalar.activation(hh[:, m % HSLOTS], hf[:, m % 2], ACT.Copy).then_inc(s_hh, 1)
                    if m == 4:
                        ahead(s + 1)
                boundary(s + 1)

            def h_hi(r, f):
                act.wait_ge(s_hf3, r * F3 + f + 1)
                if f >= HSLOTS:
                    act.wait_ge(s_down3, r * F3 + f - HSLOTS + 1)
                nc.scalar.activation(hh[:, f % HSLOTS], hf[:, f % 2], ACT.Copy).then_inc(s_hh3, 1)

            def group3(r, last=False):
                act.wait_ge(s_lg, r + 1)
                nc.scalar.activation(ltf[:], p_pre[0][0:2 * E3, :], ACT.Copy).then_inc(s_ltf, 1)
                act.wait_ge(s_dd, r + 1)
                nc.scalar.activation(rt[:, 100:108], rt[:, 92:100], ACT.Exp).then_inc(s_ee, 1)
                for f in range(F3):
                    if f == 2:
                        act.wait_ge(s_gt, r + 1)
                        nc.scalar.activation(gts[:], p_acc[0][0:ES, :], ACT.Copy).then_inc(s_gth, 1)
                        for e in range(E3):
                            act.wait_ge(s_gb, r * E3 + e + 1)
                            nc.scalar.activation(gbc[:, e], p_acc[e + 1][:], ACT.Copy).then_inc(s_gbc, 1)
                        for g in range(2):
                            h_hi(r, g)
                    fn = (ACT.Tanh, ACT.Gelu, ACT.Silu)[f // FT]
                    act.wait_ge(s_pre, r * F3 + f + 1)
                    if f >= 2:
                        act.wait_ge(s_hl3, r * F3 + f - 1)
                    nc.scalar.activation(sil[:, f % 2], p_pre[(f + 1) % 4][:], fn, bias=b1c[:, f:f + 1]).then_inc(s_act, 1)
                    if f >= 2:
                        h_hi(r, f)
                    if f == 8 and not last:
                        ahead(r + GROUPS + 1)
                if not last:
                    boundary(r + GROUPS + 1)

            with act.Fori(0, GROUPS - 1) as r:
                group3(r)
            group3(GROUPS - 1, True)

        @block.vector
        def _(dve):
            v = nc.vector
            chain = Chain(dve, ch_set)

            dve.wait_ge(d_cond, 48)
            dve.wait_ge(s_ctx, 1)
            v.tensor_tensor(ctxs[:], bank[6][0:BATCH, 256:256 + CH], fsb[:], ALU.add).then_inc(s_ctxs, 1)
            dve.wait_ge(s_ctxs, 2)
            v.tensor_tensor(ctxp[:, 1], ctxs[:], ctxp[:, 0].bitcast(F32), ALU.subtract).then_inc(s_ctxs, 1)
            dve.wait_ge(s_cvs, 1)
            v.tensor_tensor(cvl, conv_raw[:], cvh.bitcast(F32), ALU.subtract).then_inc(s_cvs, 1)
            dve.wait_ge(s_m3, 1)
            dve.wait_ge(d_mlp, 64)
            logits = bank[6][0:BATCH, 0:COND_LAYERS * MIX].rearrange("p (l k) -> p l k", k=MIX)

            def rows(n):
                return attm[:, n, :].unsqueeze(2).to_broadcast([BATCH, COND_LAYERS, MIX])

            chain.link(v.tensor_tensor(att[:], logits, mb2[:], ALU.add))
            chain.link(v.tensor_reduce(attm[:, 0, :], att[:], AX.X, ALU.max))
            v.tensor_tensor(att[:], att[:], rows(0), ALU.subtract).then_inc(s_lm, 1)
            dve.wait_ge(s_w0s, 1)
            v.tensor_tensor(w0l[:], w0_raw[:], w0h[:].bitcast(F32), ALU.subtract).then_inc(s_w0s, 1)

            def t0_rows(t):
                for h in range(2):
                    dve.wait_ge(s_cvx, 2 * t + h + 1)
                    v.tensor_tensor(t0f[:, :, h * P // 2:(h + 1) * P // 2], p_cv[h][:, 0:256].rearrange("p (a n) -> p a n", a=PH),
                                    cvx[:, h].rearrange("p (a n) -> p a n", a=PH), ALU.add).then_inc(s_t0f, 1)
                dve.wait_ge(s_t0h, t + 1)
                v.tensor_tensor(t0l[:], t0f[:], t0h[:].bitcast(F32), ALU.subtract).then_inc(s_t0l, 1)

            t0_rows(0)
            dve.wait_ge(s_ex, 1)
            chain.link(v.tensor_reduce(attm[:, 1, :], atte[:], AX.X, ALU.add))
            chain.link(v.reciprocal(attm[:, 2, :], attm[:, 1, :]))
            v.tensor_tensor(att[:], atte[:], rows(2), ALU.mult).then_inc(s_at, 1)
            dve.wait_ge(d_w1, 16)
            chain.link(v.tensor_reduce(wsc[:, 0, :], w1_raw[:], AX.X, ALU.max, apply_absolute_value=True))
            chain.link(v.tensor_scalar(wsc[:, 1, :], wsc[:, 0, :], 1.0 / QMAX, QEPS, ALU.mult, ALU.max))
            v.reciprocal(wsc[:, 2, :], wsc[:, 1, :]).then_inc(s_sw, 1)
            gate, quant = Chain(dve, ch_gate), Chain(dve, ch_q)
            GATE_LINKS, QUANT_LINKS = 9, 4

            def integers(t, later2=True):
                quant.begin((t - 1) * QUANT_LINKS)
                dve.wait_ge(s_c1, t)
                quant.link(v.tensor_reduce(sx[:, 0:1], c1[:], AX.X, ALU.max, apply_absolute_value=True))
                quant.link(v.tensor_scalar(sx[:, 1:2], sx[:, 0:1], 1.0 / QMAX, QEPS, ALU.mult, ALU.max))
                quant.link(v.reciprocal(sx[:, 2:3], sx[:, 1:2]))
                quant.link(v.tensor_scalar(c1[:], c1[:], sx[:, 2:3], MAGIC, ALU.mult, ALU.add))
                assert quant.k == QUANT_LINKS
                if later2:
                    dve.wait_ge(s_qt, t - 1)
                v.tensor_scalar(qb[:], c1[:], MAGIC, QMAX, ALU.subtract, ALU.min).then_inc(s_qb, 1)

            def scaled_back(t, later2=True):
                dve.wait_ge(s_y1, t)
                dve.wait_ge(d_swb, 16)
                if later2:
                    dve.wait_ge(s_x2, t - 1)
                v.scalar_tensor_tensor(yt[:], p_y1[:], sx[:, 1:2], swb[:], ALU.mult, ALU.mult).then_inc(s_yt, 1)

            def step(t, p, own, conv=True):
                later = not (isinstance(t, int) and t == 0)
                later2 = not (isinstance(t, int) and t <= 1)
                gate.begin(t * GATE_LINKS)
                dve.wait_ge(s_ga, t + 1)
                gate.link(v.tensor_copy(lg[:], p_ga[:, ER:ER + E0]))
                v.tensor_reduce(gs[:, 2:3], lg[:], AX.X, ALU.max)
                gate.link(v.max(mx8[:], lg[:]))
                v.tensor_tensor(gs[:, 3:4], mx8[:, 1:2], gs[:, 2:3], ALU.subtract).then_inc(s_gd, 1)
                gate.link(v.max_index(ix8[:], mx8[:], lg[:]))
                gate.link(v.tensor_copy(gs[:, 0:2], ix8[:, 0:2]))
                dve.wait_ge(s_ge, t + 1)
                gate.link(v.tensor_scalar(gs[:, 5:6], gs[:, 4:5], 1.0, 1.0 / LORA_SCALE, ALU.add, ALU.mult))
                gate.link(v.reciprocal(gs[:, 6:7], gs[:, 5:6]))
                gate.link(v.tensor_tensor(gs[:, 7:8], gs[:, 4:5], gs[:, 6:7], ALU.mult))
                v.tensor_scalar(g0[:, 0], iota[:], gs[:, 0:1], gs[:, 6:7], ALU.is_equal, ALU.mult)
                gate.link(v.tensor_scalar(g0[:, 1], iota[:], gs[:, 1:2], gs[:, 7:8], ALU.is_equal, ALU.mult))
                gate.link(v.tensor_tensor(g0[:, 2], g0[:, 0], g0[:, 1], ALU.add))
                assert gate.k == GATE_LINKS
                v.tensor_tensor(hm[:].rearrange("p (e r) -> p e r", r=RANK),
                                p_ga[:, 0:ER].rearrange("p (e r) -> p e r", r=RANK),
                                g0[:, 2].unsqueeze(2).to_broadcast([P, E0, RANK]), ALU.mult).then_inc(s_hm, 1)
                dve.wait_ge(s_hmh, t + 1)
                v.tensor_tensor(hml[:], hm[:], hmh[:].bitcast(F32), ALU.subtract).then_inc(s_hml, 1)
                if later:
                    if not later2:
                        for k in range(KT):
                            dve.wait_ge(s_wqt, k // 2 * 2 + 2)
                            v.tensor_copy(wq[:, k], bank[6 - k // 2][:].bitcast(BF16)[:, (k % 2) * D:(k % 2 + 1) * D]).then_inc(s_wqc, 1)
                    integers(t, later2)
                else:
                    dve.wait_ge(s_sw, 1)
                    for k in range(KT):
                        chain.link(v.tensor_scalar(w1_raw[:, k], w1_raw[:, k], wsc[:, 2, k:k + 1], MAGIC, ALU.mult, ALU.add))
                        v.tensor_scalar(wq_rows[:, k], w1_raw[:, k], MAGIC, QMAX, ALU.subtract, ALU.min).then_inc(s_wqr, 1)
                if conv:
                    t0_rows(t + 1)
                dve.wait_ge(s_y0, t + 1)
                dve.wait_ge(d_xin[p], own * 16)
                if later:
                    dve.wait_ge(s_x1h, t)
                    dve.wait_ge(s_x1l, t)
                    dve.wait_ge(s_x1b, t)
                v.tensor_tensor(x1[:], p_y0[:], xin[:, p], ALU.add).then_inc(s_x1, 1)
                if later:
                    scaled_back(t, later2)

            step(0, 0, 1)
            dve.wait_ge(s_l3s, 2)
            v.tensor_tensor(gwp[:, :, E3:2 * E3], gw_raw[:], gwp[:, :, 0:E3].bitcast(F32), ALU.subtract).then_inc(s_l3s, 1)
            v.tensor_tensor(b2s[64:ES], b2_raw[64:ES], b2s[64:ES].bitcast(F32), ALU.subtract).then_inc(s_l3s, 1)
            step(1, 1, 1)
            step(2, 0, 2)
            with dve.Fori(1, 6) as i:
                step(i * 2 + 1, 1, i + 1)
                step(i * 2 + 2, 0, i + 2)
            step(13, 1, 7)
            step(14, 0, 8)
            step(15, 1, 8, conv=False)

            def x_lo(c):
                for j in (2, 3):
                    dve.wait_ge(s_xch, c * GT + j + 1)
                    v.tensor_tensor(xcl[:, j % 2], xc[:, j % 2], xch[:, j % 2].bitcast(F32), ALU.subtract).then_inc(s_xcld, 1)

            def t_rows(c):
                dve.wait_ge(s_cond, (c + 1) * GT)
                dve.wait_ge(d_bias, (c + 1) * 16)

                def lo(kt):
                    dve.wait_ge(s_th, c * KT + kt + 1)
                    v.tensor_tensor(tl[:, kt], tf[:, kt], th[:, kt].bitcast(F32), ALU.subtract).then_inc(s_tld, 1)

                for kt in range(KT):
                    v.tensor_tensor(tf[:, kt], p_pre[kt][:], bias23[:], ALU.add).then_inc(s_tf, 1)
                    if kt == 2:
                        lo(1)
                lo(3)

            def residual(c, done, value):
                dve.wait_ge(done, value)
                dve.wait_ge(d_xres, (c + 1) * 16)
                for j in (3, 2, 1, 0):
                    v.tensor_tensor(xres[:, j], p_acc[j][:], xres[:, j], ALU.add).then_inc(s_res, 1)

            x_lo(0)
            integers(TILES)
            t_rows(0)
            scaled_back(TILES)
            with dve.Fori(0, GROUPS) as s:
                for m in range(MT):
                    dve.wait_ge(s_up, s * MT + m + 1)
                    dve.wait_ge(s_sil, s * MT + m + 1)
                    v.tensor_tensor(hf[:, m % 2], p_pre[2 * (m % 2) + 1][:], sil[:, m % 2], ALU.mult).then_inc(s_hf, 1)
                    dve.wait_ge(s_hh, s * MT + m + 1)
                    v.tensor_tensor(hl[:, m % HSLOTS], hf[:, m % 2], hh[:, m % HSLOTS].bitcast(F32), ALU.subtract).then_inc(s_hl, 1)
                x_lo(s + 1)
                t_rows(s + 1)
                residual(s, s_down, (s + 1) * MT)

            route = Chain(dve, ch_rt)

            def col(n, w=GT):
                return rt[:, n:n + w]

            LL, RB, G, NG, I1, I3 = 0, 24, 36, 48, 60, 72
            DD, EE = 92, 100
            TMP = 140

            def three(n):
                return rt[:, n:n + E3 * GT].rearrange("p (e j) -> p e j", e=E3)

            dve.wait_ge(s_down, MT * GROUPS)
            v.memset(gp[:], 0.0).then_inc(s_gp, 1)

            def strengths(r):
                tok = tf[:].rearrange("p k (b s) -> p k b s", s=CH)
                dve.wait_ge(s_tf, (r + GROUPS + 1) * KT)
                v.tensor_reduce(rs[:, 0], tok[:, :, :, 0:VIS], AX.X, ALU.add, apply_absolute_value=True).then_inc(s_rs, 1)
                v.tensor_reduce(rs[:, 1], tok[:, :, :, VIS:CH], AX.X, ALU.add, apply_absolute_value=True).then_inc(s_rs, 1)

            strengths(0)

            def group3(r, last=False):
                route.begin(r * ROUTE_LINKS)
                dve.wait_ge(s_lgt, r + 1)
                v.tensor_copy(three(LL), p_acc[2][:, 0:GT * 4].rearrange("p (j e) -> p e j", e=4)[:, 0:E3, :]).then_inc(s_lgc, 1)
                dve.wait_ge(s_sum, r + 1)
                route.link(v.tensor_tensor(rt[:, 200:232].rearrange("p (q b) -> p q b", b=BPT),
                                           p_acc[1][:, 0:32].rearrange("p (q b) -> p q b", b=BPT),
                                           mask4[:].unsqueeze(1).to_broadcast([P, 2 * GT, BPT]), ALU.mult))
                route.link(v.tensor_reduce(col(TMP, 8), rt[:, 200:232].rearrange("p (q b) -> p q b", b=BPT), AX.X, ALU.add))
                route.link(v.tensor_scalar(col(TMP + 8), col(TMP), 1.0 / (VIS * D), 1e-8, ALU.mult, ALU.add))
                route.link(v.reciprocal(col(TMP + 12), col(TMP + 8)))
                route.link(v.scalar_tensor_tensor(col(TMP + 16), col(TMP + 4), 1.0 / ((CH - VIS) * D), col(TMP + 12),
                                                  ALU.mult, ALU.mult))
                for e in range(E3):
                    ins = v.tensor_scalar(col(RB + GT * e), col(TMP + 16), gwb[:, e:e + 1], gbb[:, e:e + 1], ALU.mult, ALU.add)
                route.link(ins)
                dve.wait_ge(s_lgc, r + 1)
                dve.wait_ge(s_stat, r + 1)
                v.tensor_tensor(col(LL, 12), col(LL, 12), col(RB, 12), ALU.add)
                route.link(v.tensor_tensor(col(LL + 12, 12), p_acc[2][:, 32:44], col(RB, 12), ALU.add))
                a, b, c_ = (col(LL + GT * e) for e in range(E3))
                v.tensor_tensor(col(TMP + 20), a, b, ALU.max)
                route.link(v.tensor_tensor(col(TMP + 24), a, b, ALU.min))
                v.tensor_tensor(col(TMP + 28), col(TMP + 20), c_, ALU.max)
                route.link(v.tensor_tensor(col(TMP + 32), col(TMP + 20), c_, ALU.min))
                v.tensor_tensor(col(TMP + 36), col(TMP + 24), col(TMP + 32), ALU.max)
                route.link(v.tensor_tensor(col(TMP + 40), col(TMP + 24), c_, ALU.min))
                v.tensor_tensor(rt[:, DD:DD + 8].rearrange("p (q j) -> p q j", q=2),
                                rt[:, TMP + 36:TMP + 44].rearrange("p (q j) -> p q j", q=2),
                                col(TMP + 28).unsqueeze(1).to_broadcast([P, 2, GT]), ALU.subtract).then_inc(s_dd, 1)
                a0, b0, c0 = (col(LL + 12 + GT * e) for e in range(E3))
                ab, ac, bc = (col(G + GT * n) for n in range(3))
                nab, nac, nbc = (col(NG + GT * n) for n in range(3))
                v.tensor_tensor(ab, a0, b0, ALU.is_ge)
                v.tensor_tensor(ac, a0, c0, ALU.is_ge)
                route.link(v.tensor_tensor(bc, b0, c0, ALU.is_ge))
                route.link(v.tensor_scalar(col(NG, 12), col(G, 12), -1.0, 1.0, ALU.mult, ALU.add))
                for n, (x, y) in enumerate(((ab, ac), (nab, bc), (nac, nbc))):
                    v.tensor_tensor(col(I1 + GT * n), x, y, ALU.mult)
                for n, (x, y) in enumerate(((nab, nac), (ab, nbc), (ac, bc))):
                    ins = v.tensor_tensor(col(I3 + GT * n), x, y, ALU.mult)
                route.link(ins)
                route.link(v.tensor_tensor(col(NG, 12), col(I1, 12), col(I3, 12), ALU.add))
                route.link(v.tensor_scalar(col(I3, 12), col(NG, 12), -1.0, 1.0, ALU.mult, ALU.add))
                dve.wait_ge(s_ee, r + 1)
                route.link(v.tensor_scalar(col(TMP + 20), col(EE), 1.0, None, ALU.add))
                route.link(v.tensor_tensor(col(TMP + 24), col(TMP + 20), col(EE + 4), ALU.add))
                route.link(v.scalar_tensor_tensor(col(TMP + 28), col(TMP + 24), 1e-8, col(TMP + 20), ALU.mult, ALU.add))
                route.link(v.reciprocal(col(TMP + 32), col(TMP + 28)))
                route.link(v.tensor_tensor(col(TMP + 36), col(EE), col(TMP + 32), ALU.mult))
                v.tensor_tensor(three(G), three(I1), col(TMP + 32).unsqueeze(1).to_broadcast([P, E3, GT]), ALU.mult)
                route.link(v.tensor_tensor(three(NG), three(I3), col(TMP + 36).unsqueeze(1).to_broadcast([P, E3, GT]), ALU.mult))
                assert route.k == ROUTE_LINKS, route.k
                dve.wait_ge(s_gp, 1)
                for n in range(3):
                    ins = v.tensor_tensor(gp[:, :, 32 * n:32 * n + E3].rearrange("p j e -> p e j"), three(G), three(NG), ALU.add)
                ins.then_inc(s_g, 1)
                dve.wait_ge(s_gth, r + 1)
                v.tensor_tensor(gts[32:32 + E3, :], p_acc[0][32:32 + E3, :], gts[32:32 + E3, :].bitcast(F32),
                                ALU.subtract).then_inc(s_gtl, 1)
                for f in range(F3):
                    e = f // FT
                    dve.wait_ge(s_act, r * F3 + f + 1)
                    dve.wait_ge(s_gbc, r * E3 + e + 1)
                    v.tensor_tensor(hf[:, f % 2], sil[:, f % 2], gbc[:, e], ALU.mult).then_inc(s_hf3, 1)
                    dve.wait_ge(s_hh3, r * F3 + f + 1)
                    v.tensor_tensor(hl[:, f % HSLOTS], hf[:, f % 2], hh[:, f % HSLOTS].bitcast(F32), ALU.subtract).then_inc(s_hl3, 1)
                if not last:
                    x_lo(r + GROUPS + 1)
                    t_rows(r + GROUPS + 1)
                    strengths(r + 1)
                    residual(r + GROUPS, s_down3, (r + 1) * F3)
                else:
                    dve.wait_ge(d_xres, (r + GROUPS + 1) * 16)
                    for j in range(GT):
                        dve.wait_ge(s_last, j + 1)
                        v.tensor_tensor(xres[:, j], p_acc[j][:], xres[:, j], ALU.add).then_inc(s_res, 1)

            ROUTE_LINKS = 21
            with dve.Fori(0, GROUPS - 1) as r:
                group3(r)
            group3(GROUPS - 1, True)

        @block.tensor
        def _(pe):
            mm = nc.tensor.matmul

            def conv(t, h, p):
                pe.wait_ge(s_tapl, t + 1)
                if not (isinstance(t, int) and t == 0):
                    pe.wait_ge(s_t0f, 2 * t - 1 + h)
                both = p_cv[h][:].rearrange("p (a b c) -> p a b c", a=2 * PH, b=BPT // 2)
                for b in range(BPT // 2):
                    for j in range(SHIFTS):
                        mm(both[:, :, b], taph[:, 2 * h + b, j:j + P],
                           cvw[:, j].rearrange("p q (a c) -> p (q a) c", a=PH), start=(b == 0 and j == 0), stop=False,
                           skip_group_check=True)
                        mm(both[:, 0:PH, b], tapl[:, 2 * h + b, j:j + P],
                           cvh[:, j].rearrange("p (a c) -> p a c", a=PH), start=False, stop=False,
                           skip_group_check=True)
                pe.wait_ge(s_b0, t + 1)
                mm(both[:, 0:PH].rearrange("p a b c -> p a (b c)"), onesr[:],
                   bias0[:, p, h * P // 2:(h + 1) * P // 2].unsqueeze(1).to_broadcast([2, PH, P // 2]),
                   start=False, stop=True, skip_group_check=True).then_inc(s_cv, 1)

            pe.wait_ge(d_cond, 48)
            mm(bank[6][0:BATCH, 256:256 + CH], condt[:], cwt[:], start=True, stop=True).then_inc(s_ctx, 1)
            pe.wait_ge(d_mlp, 64)
            for l in range(COND_LAYERS):
                mm(bank[2][:, l * BATCH:(l + 1) * BATCH], mw01[:, l, 0], condt[:], start=True, stop=True).then_inc(s_m1, 1)
            pe.wait_ge(s_g1, COND_LAYERS)
            for l in range(COND_LAYERS):
                mm(bank[3][:, l * BATCH:(l + 1) * BATCH], mw01[:, l, 1], hid1[:, l], start=True, stop=True).then_inc(s_m2, 1)
            pe.wait_ge(s_cvs, 2)
            pe.wait_ge(s_constv, 1)
            conv(0, 0, 0)
            pe.wait_ge(s_ctxs, 1)
            pe.wait_ge(s_g2, COND_LAYERS)
            for l in range(COND_LAYERS):
                last = mm(bank[6][0:BATCH, l * MIX:(l + 1) * MIX], hid2[:, l], mw2[:, l], start=True, stop=True)
            last.then_inc(s_m3, 1)
            conv(0, 1, 0)

            def mixing_weights():
                pe.wait_ge(s_at, 1)
                pe.wait_ge(s_const, 14)
                for l in range(COND_LAYERS):
                    last = nc.tensor.transpose(bank[5][0:MIX, l * BATCH:(l + 1) * BATCH], att[:, l], ident[0:BATCH, 0:BATCH])
                last.then_inc(s_att, 1)
                pe.wait_ge(d_mix, 32)
                pe.wait_ge(s_atc, 1)
                for l in range(COND_LAYERS):
                    mm(bank[6][0:BATCH, l * CH:(l + 1) * CH], attt[:, l], mixb[:, l], start=True, stop=True)

            def mixed(l):
                if l > 0:
                    pe.wait_ge(s_agc, 3 * l)
                mm(bank[4][0:BATCH, :], attt[:, l], mixw[:, l, 0:512], start=True, stop=True)
                mm(bank[5][0:BATCH, :], attt[:, l], mixw[:, l, 512:AGW], start=True, stop=True).then_inc(s_ag, 1)

            def features(dst, weights, width, stop):
                n = 0
                for k in range(PH):
                    for x, w in ((t0h, weights[0]), (t0h, weights[1]), (t0l, weights[0])):
                        last = mm(dst[:, 0:width], x[:, k], w[:, k, :], start=(n == 0), stop=(stop and n == 3 * PH - 1),
                                  skip_group_check=not stop)
                        n += 1
                return last

            def mix1(t, slot, later2=True):
                pe.wait_ge(s_x1l, t)
                pe.wait_ge(s_bdl, t)
                if later2:
                    pe.wait_ge(s_c1, t - 1)
                for n, (w, x) in enumerate(parts((bd1h[:, slot], bd1l[:, slot]), (x1h[:], x1l[:]))):
                    last = mm(p_c1[:], w, x, start=(n == 0), stop=(n == 2))
                last.then_inc(s_cd1, 1)

            def integers_t(t, later2=True):
                pe.wait_ge(s_qb, t)
                if later2:
                    pe.wait_ge(s_qtc, t - 1)
                for k in range(KT):
                    last = nc.tensor.transpose(p_qt[:].bitcast(BF16)[:, k * P:(k + 1) * P], qb[:, k * P:(k + 1) * P], identb[:])
                last.then_inc(s_qt, 1)

            def linear1(t, later2=True):
                pe.wait_ge(s_qtc, t)
                if later2:
                    pe.wait_ge(s_yt, t - 1)
                pe.wait_ge(s_wqc, KT)
                for k in range(KT):
                    last = mm(p_y1[:], qt[:, k], wq[:, k], start=(k == 0), stop=(k == KT - 1))
                last.then_inc(s_y1, 1)

            def step(t, p, conv_=True):
                later = not (isinstance(t, int) and t == 0)
                later2 = not (isinstance(t, int) and t <= 1)
                pe.wait_ge(s_t0l, t + 1)
                if later:
                    pe.wait_ge(s_hm, t)
                features(p_ga, (gah, gal), ER + E0, True).then_inc(s_ga, 1)
                if later and not later2:
                    pe.wait_ge(s_wqr, KT)
                    pe.wait_ge(s_agc, 9)
                    for k in range(KT):
                        for o in range(KT):
                            last = nc.tensor.transpose(bank[6 - k // 2][:].bitcast(BF16)[:, (k % 2) * D + o * P:(k % 2) * D + (o + 1) * P],
                                                       wq_rows[:, o, k * P:(k + 1) * P], identb[:])
                        last.then_inc(s_wqt, 1)
                if later:
                    pe.wait_ge(s_x1, t)
                else:
                    pe.wait_ge(s_w0s, 2)
                features(p_y0, (w0h, w0l), D, False).then_inc(s_base, 1)
                if later:
                    mix1(t, 1 - p, later2)
                else:
                    mixing_weights()
                    mixed(0)
                if conv_:
                    conv(t + 1, 0, 1 - p)
                if not later:
                    mixed(1)
                    pe.wait_ge(s_constv, 3)
                pe.wait_ge(s_hml, t + 1)
                if later:
                    pe.wait_ge(s_htc, t)
                for a, src in enumerate((hmh, hml)):
                    for b in range(2):
                        last = nc.tensor.transpose(p_ht[0:HB, (2 * a + b) * P:(2 * a + b + 1) * P].bitcast(F32R),
                                                   src[:, b * HB:(b + 1) * HB], identr[:])
                last.then_inc(s_ht, 1)
                if conv_:
                    conv(t + 1, 1, 1 - p)
                if later and conv_:
                    integers_t(t, later2)
                pe.wait_ge(s_htc, t + 1)
                pe.wait_ge(s_lbs, 2)
                for b in range(2):
                    for n, (x, w) in enumerate(((hts[:, 0, b], lbh[:, b]), (hts[:, 0, b], lbl[:, b]), (hts[:, 1, b], lbh[:, b]))):
                        last = mm(p_y0[:], x, w, start=False, stop=(b == 1 and n == 2), skip_group_check=True)
                last.then_inc(s_y0, 1)
                if not later:
                    mixed(2)
                if later:
                    if not conv_:
                        integers_t(t, later2)
                    linear1(t, later2)

            pe.wait_ge(s_gas, 2)
            step(0, 0)
            step(1, 1)
            step(2, 0)
            with pe.Fori(1, 6) as i:
                step(i * 2 + 1, 1)
                step(i * 2 + 2, 0)
            step(13, 1)
            step(14, 0)
            step(15, 1, conv_=False)

            def cond(c, tiles=range(GT)):
                pe.wait_ge(s_gl, c + 1)
                for j in tiles:
                    if j < 2:
                        pe.wait_ge(s_xclp, c * 2 + j + 1)
                    else:
                        pe.wait_ge(s_xcld, c * 2 + j - 1)
                    for kt in range(KT):
                        cols = slice(kt * P, (kt + 1) * P)
                        xp = (xch[:, j % 2, cols], xcl[:, j % 2, cols])
                        for n, (x, w) in enumerate(parts(xp, (bdh[:, j], bdl[:, j]))):
                            last = mm(p_pre[kt][:, j * P:(j + 1) * P], x, w, start=(n == 0), stop=(n == 2))
                    last.then_inc(s_cond, 1)

            def wait_t(c, kt):
                pe.wait_ge(s_tld if kt % 2 else s_tlp, c * 2 + kt // 2 + 1)

            pe.wait_ge(s_x1, TILES)
            cond(0, (0, 1))
            mix1(TILES, 1)
            cond(0, (2, 3))
            integers_t(TILES)
            linear1(TILES)

            def down2(s, m):
                if m == 0:
                    pe.wait_ge(s_yt, TILES)
                pe.wait_ge(s_hl, s * MT + m + 1)
                for j in range(GT):
                    for n, h in enumerate((hh, hl)):
                        last = mm(p_acc[j][:], h[:, m % HSLOTS, j * P:(j + 1) * P], wdr[:, m],
                                  start=(m == 0 and n == 0), stop=(m == MT - 1 and n == 1), skip_group_check=True)
                last.then_inc(s_down, 1)

            with pe.Fori(0, GROUPS) as s:
                pe.wait_ge(d_w2, 16 * 3 * W2_CHUNKS)
                for m in range(MT):
                    for w, reader, done, b in ((wgr, s_sil, s_gate, 0), (wur, s_hf, s_up, 1)):
                        if m >= 2:
                            pe.wait_ge(reader, s * MT + m - 1)
                        for kt in range(KT):
                            if m == 0 and b == 0:
                                wait_t(s, kt)
                            for n, x in enumerate((th, tl)):
                                last = mm(p_pre[2 * (m % 2) + b][:], w[:, kt, m * P:(m + 1) * P], x[:, kt],
                                          start=(kt == 0 and n == 0), stop=(kt == KT - 1 and n == 1))
                        last.then_inc(done, 1)
                    if m >= LAG2:
                        down2(s, m - LAG2)
                pe.wait_ge(s_hf, (s + 1) * MT)
                cond(s + 1)
                for m in range(MT - LAG2, MT):
                    down2(s, m)

            def pre3(r, f):
                e, ft = divmod(f, FT)
                if f == 0:
                    pe.wait_ge(s_w3, 16)
                if f == 2 * FT:
                    pe.wait_ge(s_w3, 32)
                if f >= 4:
                    pe.wait_ge(s_act, r * F3 + f - 3)
                wh, wl = (w1bh, w1bl) if e == 2 else (w1ah[:, e], w1al[:, e])
                for kt in range(KT):
                    cols = slice(ft * P, (ft + 1) * P)
                    for n, (w, x) in enumerate(parts((wh[:, kt, cols], wl[:, kt, cols]), (th[:, kt], tl[:, kt]))):
                        last = mm(p_pre[(f + 1) % 4][:], w, x, start=(kt == 0 and n == 0), stop=(kt == KT - 1 and n == 2))
                last.then_inc(s_pre, 1)

            def down3(r, f, per_tile=False):
                e, ft = divmod(f, FT)
                if ft == 0:
                    pe.wait_ge(s_w3, (24, 40, 48)[e])
                pe.wait_ge(s_hl3, r * F3 + f + 1)
                for j in range(GT):
                    cols = slice(j * P, (j + 1) * P)
                    hp = (hh[:, f % HSLOTS, cols], hl[:, f % HSLOTS, cols])
                    for n, (h, w) in enumerate(parts(hp, (w2h[:, e, ft], w2l[:, e, ft]))):
                        last = mm(p_acc[j][:], h, w, start=False, stop=(f == F3 - 1 and n == 2), skip_group_check=True)
                    if per_tile:
                        last.then_inc(s_last, 1)
                if not per_tile:
                    last.then_inc(s_down3, 1)

            def group3(r, last_=False):
                c = r + GROUPS
                for kt in range(KT):
                    wait_t(c, kt)
                    mm(p_pre[0][0:2 * E3, :], gwp[:, kt], th[:, kt], start=(kt == 0), stop=(kt == KT - 1), skip_group_check=True)
                    last = mm(p_pre[0][0:E3, :], gwp[:, kt, 0:E3], tl[:, kt], start=False, stop=(kt == KT - 1),
                              skip_group_check=True)
                last.then_inc(s_lg, 1)
                pre3(r, 0)
                pe.wait_ge(s_ltf, r + 1)
                pe.wait_ge(s_res, c * GT - 2)
                for j in range(GT):
                    last = mm(p_acc[2][:, 4 * j:4 * j + E3], ltf[:, j * P:(j + 1) * P], fold[:], start=True, stop=True)
                last.then_inc(s_lgt, 1)
                pe.wait_ge(s_rs, 2 * r + 2)
                pe.wait_ge(s_res, c * GT - 1)
                for kt in range(KT):
                    last = mm(p_acc[1][:, 0:32].rearrange("p (q b) -> p q b", q=2), ones[:], rs[:, :, kt, :],
                              start=(kt == 0), stop=(kt == KT - 1))
                last.then_inc(s_sum, 1)
                pre3(r, 1)
                pe.wait_ge(s_lgc, r + 1)
                mm(p_acc[2][:, 32:44], first[:], rt[:, 0:12], start=True, stop=True).then_inc(s_stat, 1)
                pre3(r, 2)
                pre3(r, 3)
                pe.wait_ge(s_g, r + 1)
                pe.wait_ge(s_res, c * GT)
                for j in range(GT):
                    last = nc.tensor.transpose(p_acc[0][0:ES, j * P:(j + 1) * P], gp[:, j], ident[:])
                last.then_inc(s_gt, 1)
                pre3(r, 4)
                pe.wait_ge(s_gtl, r + 1)
                for e in range(E3):
                    mm(p_acc[e + 1][:], selr[:, e], gts[:], start=True, stop=True).then_inc(s_gb, 1)
                pre3(r, 5)
                pe.wait_ge(s_gbc, (r + 1) * E3)
                for j in range(GT):
                    mm(p_acc[j][:], gts[:, j * P:(j + 1) * P], b2s[:], start=True, stop=False, skip_group_check=True)
                down3(r, 0)
                for f in range(LAG3 + 1, F3):
                    pre3(r, f)
                    down3(r, f - LAG3)
                down3(r, F3 - LAG3)
                if not last_:
                    pe.wait_ge(s_act, (r + 1) * F3)
                    cond(c + 1, (0, 1))
                down3(r, F3 - LAG3 + 1)
                if not last_:
                    cond(c + 1, (2, 3))
                for f in range(F3 - LAG3 + 2, F3):
                    down3(r, f, last_ and f == F3 - 1)

            with pe.Fori(0, GROUPS - 1) as r:
                group3(r)
            group3(GROUPS - 1, True)


_ORDER = ["x_rows", "x_taps", "cond_t", "fside", "cw_t", "conv_w", "l0_w", "l0_ga", "l0_lb",
          "mlp_w01", "mlp_w2", "mlp_b01", "mlp_b2", "mix_w", "mix_b", "l1_w", "l1_b",
          "wg", "wu", "wd", "gate_w", "gate_w_last", "gate_b", "w1", "b1", "w2", "b2"]


def kernel(**inputs):
    import numpy as _np
    import concourse.bacc as _bacc
    from concourse import mybir as _mybir
    from concourse.bass_utils import run_bass_kernel_spmd as _run

    v = {k: _np.asarray(a) for k, a in inputs.items()}

    def tiled(a):
        return a.reshape(a.shape[0] // P, P, *a.shape[1:]).swapaxes(0, 1)

    padded = _np.zeros((BATCH, CH, PH * MW), v["x"].dtype)
    padded[:, :, PH:PH + D] = v["x"]
    x_taps = padded.reshape(BATCH, CH, MW, PH).transpose(3, 1, 0, 2).reshape(P, BATCH, MW)
    w = v["L0_cond_weight"]
    gc = CH // CONV_GROUPS
    conv_w = _np.zeros((PH, CH, SHIFTS, PH, CH), w.dtype)
    for s in range(PH):
        for j in range(SHIFTS):
            for p in range(PH):
                if 0 <= PH * j + s - p < TAPS:
                    for g in range(CONV_GROUPS):
                        o = slice(g * gc, (g + 1) * gc)
                        conv_w[s, o, j, p, o] = w[o, :, PH * j + s - p].T
    lora_a = v["L0_ffn_lora_A"].reshape(ER, D)
    names = [f"L{l}_cond_" for l in (1, 2, 3)]
    host = {
        "x_rows": v["x"].reshape(TILES, P, D),
        "x_taps": x_taps,
        "cond_t": v["cond_128"].T,
        "fside": v["fside_S_0"],
        "cw_t": v["L0_cond_c_weight"].T,
        "conv_w": conv_w.reshape(P, SHIFTS, P),
        "l0_w": v["L0_ffn_base_W"].reshape(D, P, PH).transpose(1, 2, 0),
        "l0_ga": _np.concatenate([lora_a, v["L0_ffn_gate_W"]]).reshape(ER + E0, P, PH).transpose(1, 2, 0),
        "l0_lb": v["L0_ffn_lora_B"].transpose(0, 2, 1).reshape(2, HB, D).transpose(1, 0, 2),
        "mlp_w01": _np.stack([_np.stack([v[n + "W0"], v[n + "W1"]], 1) for n in names], 1),
        "mlp_w2": _np.stack([v[n + "W2"] for n in names], 1),
        "mlp_b01": _np.stack([_np.stack([v[n + "b0"], v[n + "b1"]], 1) for n in names], 1),
        "mlp_b2": _np.stack([v[n + "b2"] for n in names]),
        "mix_w": _np.stack([v[n + "weight"][..., 0].transpose(0, 2, 1).reshape(MIX, AGW) for n in names], 1),
        "mix_b": _np.stack([v[n + "bias_k"] for n in names], 1),
        "l1_w": tiled(v["L1_ffn_w"]),
        "l1_b": v["L1_ffn_b"],
        "wg": tiled(v["L2_ffn_W_gate"].T),
        "wu": tiled(v["L2_ffn_W_up"].T),
        "wd": tiled(v["L2_ffn_W_down"].T),
        "gate_w": tiled(v["L3_ffn_gate_w"][:D]),
        "gate_w_last": v["L3_ffn_gate_w"][D],
        "gate_b": v["L3_ffn_gate_b"],
        "w1": v["L3_ffn_w1"].reshape(E3, KT, P, D).transpose(2, 0, 1, 3),
        "b1": v["L3_ffn_b1"].reshape(F3, P).T,
        "w2": v["L3_ffn_w2"].reshape(E3, FT, P, D).transpose(2, 0, 1, 3),
        "b2": v["L3_ffn_b2"],
    }

    nc = _bacc.Bacc("TRN2", target_bir_lowering=False, num_devices=1)
    arrays, args = {}, []
    for name in _ORDER:
        a = _np.ascontiguousarray(host[name])
        arrays[f"in_{name}_dram"] = a
        args.append(nc.dram_tensor(f"in_{name}_dram", a.shape, _mybir.dt.from_np(a.dtype), kind="ExternalInput").ap())
    out = nc.dram_tensor("out_0_dram", (TILES, P, D), F32, kind="ExternalOutput").ap()
    build(nc, *args, out)
    r = _run(nc, [arrays], core_ids=[0])
    return r.results[0]["out_0_dram"].reshape(BATCH, CH, D)
```
